# Optimizing a Trainium2 kernel written in Bass

```python
import numpy as np
import jax
import jax.numpy as jnp

def _softmax(x, axis=-1):
    return jax.nn.softmax(x, axis=axis)

def _gelu(x):
    return jax.nn.gelu(x, approximate=True)

def _silu(x):
    return jax.nn.silu(x)

def _sigmoid(x):
    return jax.nn.sigmoid(x)

def _layernorm(x, axis=-1, eps=1e-05):
    m = jnp.mean(x, axis=axis, keepdims=True)
    v = jnp.var(x, axis=axis, keepdims=True)
    return (x - m) / jnp.sqrt(v + eps)

def _scatter_add(tgt, idx, src, axis=0):
    return tgt.at[idx].add(src)

def _segment_sum(src, seg, n):
    return jax.ops.segment_sum(src, seg, n)
kernel_name = 'mk_decoder_preln_d1_seqx_r8_c8e0a4'

def setup_inputs(seed: int=0):
    np.random.seed(seed)
    _w = jnp.asarray

    def _rec_inputs():
        import jax
        import jax.numpy as jnp
        _rk = jax.random.key(seed)
        x = -7.109e-05 + 0.9999 * jax.random.normal(jax.random.fold_in(_rk, 1), (32, 128, 128), jnp.float32)
        _lenS = 128 - jax.random.randint(jax.random.fold_in(_rk, 7), (32,), 0, max(1, 128 // 4) + 1, jnp.int32)
        _lenS2 = 128 - jax.random.randint(jax.random.fold_in(_rk, 8), (32,), 0, max(1, 128 // 4) + 1, jnp.int32)
        _ctx_768P = jax.random.normal(jax.random.fold_in(_rk, 11), (32, 16, 96), jnp.float32)
        _ctx_768c = jax.random.dirichlet(jax.random.fold_in(_rk, 511), 0.3 * jnp.ones((16,), jnp.float32), (32, 128))
        _ctx_768t = jnp.einsum('bsk,bkd->bsd', _ctx_768c, _ctx_768P)
        _ctx_768t = _ctx_768t * jax.lax.rsqrt(jnp.mean(jnp.square(_ctx_768t)) + 1e-12) * 0.953939
        ctx_768 = 0.000486113 + 1.00014 * (_ctx_768t + 0.3 * jax.random.normal(jax.random.fold_in(_rk, 611), (32, 128, 96), jnp.float32))
        return (x, ctx_768)
    x, ctx_768 = _rec_inputs()

    def _L0_attn_setup():
        import jax, jax.numpy as jnp
        import numpy as np
        B, N, HID = (8, 512, 128)
        HEADS = 16
        D = HID // HEADS
        LN_EPS = 1e-05
        key = jax.random.key(seed)
        ks = jax.random.split(key, 8)
        s = 1.0 / np.sqrt(HID)
        x = jax.random.normal(ks[0], (B, N, HID), dtype=jnp.float32)
        Wh = jax.random.uniform(ks[1], (HID, HID), jnp.float32, -s, s)
        Wq = jax.random.uniform(ks[2], (HID, HID), jnp.float32, -s, s)
        Wk = jax.random.uniform(ks[3], (HID, HID), jnp.float32, -s, s)
        Wv = jax.random.uniform(ks[4], (HID, HID), jnp.float32, -s, s)
        Wo = jax.random.uniform(ks[5], (HID, HID), jnp.float32, -s, s)
        bh = jax.random.uniform(ks[6], (HID,), jnp.float32, -s, s)
        bq = jnp.zeros((HID,), jnp.float32)
        bk = jnp.zeros((HID,), jnp.float32)
        bv = jnp.zeros((HID,), jnp.float32)
        bo = jax.random.uniform(ks[7], (HID,), jnp.float32, -s, s)
        beta = jnp.full((HID,), 0.1, jnp.float32)
        ln_w = jnp.ones((HID,), jnp.float32)
        ln_b = jnp.zeros((HID,), jnp.float32)
        return {'x': x, 'Wh': Wh, 'bh': bh, 'Wq': Wq, 'bq': bq, 'Wk': Wk, 'bk': bk, 'Wv': Wv, 'bv': bv, 'beta': beta, 'ln_w': ln_w, 'ln_b': ln_b, 'Wo': Wo, 'bo': bo}
    _L0_attn_all = _L0_attn_setup()
    _L0_attn_in = {k: v for k, v in _L0_attn_all.items() if k in ('Wh', 'bh', 'Wq', 'bq', 'Wk', 'bk', 'Wv', 'bv', 'beta', 'ln_w', 'ln_b', 'Wo', 'bo')}
    del _L0_attn_all

    def _L0_xattn_setup():
        import jax, jax.numpy as jnp
        import numpy as np
        HEADS = 16
        DIM_HEAD = 64
        key = jax.random.key(seed)
        ks = jax.random.split(key, 8)
        B, S, D = (16, 512, 128)
        K, DE = (77, 96)
        inner = HEADS * DIM_HEAD
        hidden_states = jax.random.normal(ks[0], (B, S, D), dtype=jnp.float32)
        encoder_hidden_states = jax.random.normal(ks[1], (B, K, DE), dtype=jnp.float32)
        sc_q = 1.0 / np.sqrt(D)
        sc_kv = 1.0 / np.sqrt(DE)
        sc_o = 1.0 / np.sqrt(inner)
        Wq = jax.random.normal(ks[2], (D, inner), dtype=jnp.float32) * sc_q
        Wk = jax.random.normal(ks[3], (DE, inner), dtype=jnp.float32) * sc_kv
        Wv = jax.random.normal(ks[4], (DE, inner), dtype=jnp.float32) * sc_kv
        Wo = jax.random.normal(ks[5], (inner, D), dtype=jnp.float32) * sc_o
        bo = jax.random.normal(ks[6], (D,), dtype=jnp.float32) * 0.01
        return {'hidden_states': hidden_states, 'encoder_hidden_states': encoder_hidden_states, 'Wq': Wq, 'Wk': Wk, 'Wv': Wv, 'Wo': Wo, 'bo': bo}
    _L0_xattn_all = _L0_xattn_setup()
    _L0_xattn_in = {k: v for k, v in _L0_xattn_all.items() if k in ('Wq', 'Wk', 'Wv', 'Wo', 'bo')}
    del _L0_xattn_all

    def _L0_ffn_setup():
        import jax, jax.numpy as jnp
        import numpy as np
        H = 128
        I = 256
        E = 8
        B, S = (2, 128)

        def _swiglu(x, wg, wu, wd):
            return jax.nn.silu(x @ wg) * (x @ wu) @ wd
        key = jax.random.key(seed)
        ks = jax.random.split(key, 8)
        sc_h = 1.0 / np.sqrt(H)
        sc_i = 1.0 / np.sqrt(I)
        return {'hidden_states': jax.random.normal(ks[0], (B, S, H), jnp.float32), 'gate_w': jax.random.normal(ks[1], (H, E), jnp.float32) * sc_h, 'sh_gate': jax.random.normal(ks[2], (H, I), jnp.float32) * sc_h, 'sh_up': jax.random.normal(ks[3], (H, I), jnp.float32) * sc_h, 'sh_down': jax.random.normal(ks[4], (I, H), jnp.float32) * sc_i, 'rt_gate': jax.random.normal(ks[5], (E, H, I), jnp.float32) * sc_h, 'rt_up': jax.random.normal(ks[6], (E, H, I), jnp.float32) * sc_h, 'rt_down': jax.random.normal(ks[7], (E, I, H), jnp.float32) * sc_i}
    _L0_ffn_all = _L0_ffn_setup()
    _L0_ffn_in = {k: v for k, v in _L0_ffn_all.items() if k in ('gate_w', 'sh_gate', 'sh_up', 'sh_down', 'rt_gate', 'rt_up', 'rt_down')}
    del _L0_ffn_all
    return {'x': x, 'ctx_768': ctx_768, 'L0_attn_Wh': _L0_attn_in['Wh'], 'L0_attn_bh': _L0_attn_in['bh'], 'L0_attn_Wq': _L0_attn_in['Wq'], 'L0_attn_bq': _L0_attn_in['bq'], 'L0_attn_Wk': _L0_attn_in['Wk'], 'L0_attn_bk': _L0_attn_in['bk'], 'L0_attn_Wv': _L0_attn_in['Wv'], 'L0_attn_bv': _L0_attn_in['bv'], 'L0_attn_beta': _L0_attn_in['beta'], 'L0_attn_ln_w': _L0_attn_in['ln_w'], 'L0_attn_ln_b': _L0_attn_in['ln_b'], 'L0_attn_Wo': _L0_attn_in['Wo'], 'L0_attn_bo': _L0_attn_in['bo'], 'L0_xattn_Wq': _L0_xattn_in['Wq'], 'L0_xattn_Wk': _L0_xattn_in['Wk'], 'L0_xattn_Wv': _L0_xattn_in['Wv'], 'L0_xattn_Wo': _L0_xattn_in['Wo'], 'L0_xattn_bo': _L0_xattn_in['bo'], 'L0_ffn_gate_w': _L0_ffn_in['gate_w'], 'L0_ffn_sh_gate': _L0_ffn_in['sh_gate'], 'L0_ffn_sh_up': _L0_ffn_in['sh_up'], 'L0_ffn_sh_down': _L0_ffn_in['sh_down'], 'L0_ffn_rt_gate': _L0_ffn_in['rt_gate'], 'L0_ffn_rt_up': _L0_ffn_in['rt_up'], 'L0_ffn_rt_down': _L0_ffn_in['rt_down']}

def reference(x, ctx_768, L0_attn_Wh, L0_attn_bh, L0_attn_Wq, L0_attn_bq, L0_attn_Wk, L0_attn_bk, L0_attn_Wv, L0_attn_bv, L0_attn_beta, L0_attn_ln_w, L0_attn_ln_b, L0_attn_Wo, L0_attn_bo, L0_xattn_Wq, L0_xattn_Wk, L0_xattn_Wv, L0_xattn_Wo, L0_xattn_bo, L0_ffn_gate_w, L0_ffn_sh_gate, L0_ffn_sh_up, L0_ffn_sh_down, L0_ffn_rt_gate, L0_ffn_rt_up, L0_ffn_rt_down):
    import jax
    import jax.numpy as jnp

    def _L0_attn_ref(x, Wh, bh, Wq, bq, Wk, bk, Wv, bv, beta, ln_w, ln_b, Wo, bo):
        import jax, jax.numpy as jnp
        import numpy as np
        B, N, HID = (8, 512, 128)
        HEADS = 16
        D = HID // HEADS
        LN_EPS = 1e-05
        b, n, _ = x.shape
        h = x @ Wh + bh
        q = jax.nn.sigmoid(x @ Wq + bq).reshape(b, n, D, HEADS)
        k = jax.nn.sigmoid(x @ Wk + bk).reshape(b, n, D, HEADS)
        v = (x @ Wv + bv).reshape(b, n, D, HEADS)
        kv = jnp.einsum('bndh,bnmh->bdmh', k, v)
        num = jnp.einsum('bndh,bdmh->bnmh', q, kv)
        k_sum = jnp.einsum('bndh->bdh', k)
        den = jnp.einsum('bndh,bdh->bnh', q, k_sum)[:, :, None, :]
        attn = (num / den).reshape(b, n, HEADS * D)
        mu = jnp.mean(attn, axis=-1, keepdims=True)
        var = jnp.var(attn, axis=-1, keepdims=True)
        ln = (attn - mu) * jax.lax.rsqrt(var + LN_EPS) * ln_w + ln_b
        gated = ln * (h + beta)
        out = jax.nn.relu(gated @ Wo + bo)
        return out

    def _L0_xattn_ref(hidden_states, encoder_hidden_states, Wq, Wk, Wv, Wo, bo):
        import jax, jax.numpy as jnp
        import numpy as np
        HEADS = 16
        DIM_HEAD = 64
        B, S, D = hidden_states.shape
        K = encoder_hidden_states.shape[1]
        H, Dh = (HEADS, DIM_HEAD)
        scale = 1.0 / np.sqrt(Dh)
        q = hidden_states @ Wq
        k = encoder_hidden_states @ Wk
        v = encoder_hidden_states @ Wv
        q = q.reshape(B, S, H, Dh).transpose(0, 2, 1, 3)
        k = k.reshape(B, K, H, Dh).transpose(0, 2, 1, 3)
        v = v.reshape(B, K, H, Dh).transpose(0, 2, 1, 3)
        scores = jnp.einsum('bhsd,bhkd->bhsk', q, k) * scale
        probs = jax.nn.softmax(scores, axis=-1)
        out = jnp.einsum('bhsk,bhkd->bhsd', probs, v)
        out = out.transpose(0, 2, 1, 3).reshape(B, S, H * Dh)
        out = out @ Wo + bo
        return out

    def _L0_ffn_ref(hidden_states, gate_w, sh_gate, sh_up, sh_down, rt_gate, rt_up, rt_down):
        import jax, jax.numpy as jnp
        import numpy as np
        H = 128
        I = 256
        E = 8
        B, S = (2, 128)

        def _swiglu(x, wg, wu, wd):
            return jax.nn.silu(x @ wg) * (x @ wu) @ wd
        b, s, h = hidden_states.shape
        x = hidden_states.reshape(-1, h)
        logits = x @ gate_w
        top_val = jnp.max(logits, axis=-1, keepdims=True)
        top_id = jnp.argmax(logits, axis=-1)
        score = jax.nn.sigmoid(top_val)
        xs = x * score
        g = jnp.einsum('th,ehi->eti', xs, rt_gate)
        u = jnp.einsum('th,ehi->eti', xs, rt_up)
        act = jax.nn.silu(g) * u
        y = jnp.einsum('eti,eih->eth', act, rt_down)
        onehot = jax.nn.one_hot(top_id, E, dtype=x.dtype)
        routed = jnp.einsum('eth,te->th', y, onehot)
        shared = _swiglu(x, sh_gate, sh_up, sh_down)
        return (shared + routed).reshape(b, s, h)
    x = x + _L0_attn_ref(_layernorm(x, axis=-1), L0_attn_Wh, L0_attn_bh, L0_attn_Wq, L0_attn_bq, L0_attn_Wk, L0_attn_bk, L0_attn_Wv, L0_attn_bv, L0_attn_beta, L0_attn_ln_w, L0_attn_ln_b, L0_attn_Wo, L0_attn_bo)
    x = x + _L0_xattn_ref(_layernorm(x, axis=-1), ctx_768, L0_xattn_Wq, L0_xattn_Wk, L0_xattn_Wv, L0_xattn_Wo, L0_xattn_bo)
    x = x + _L0_ffn_ref(_layernorm(x, axis=-1), L0_ffn_gate_w, L0_ffn_sh_gate, L0_ffn_sh_up, L0_ffn_sh_down, L0_ffn_rt_gate, L0_ffn_rt_up, L0_ffn_rt_down)
    return x

_drawn_inputs = setup_inputs


def setup_inputs(seed=0):
    import zlib

    import numpy as np

    out = dict(_drawn_inputs(seed))
    spreads = {'L0_attn_bq': (0.0, 2.0),
     'L0_attn_bk': (0.0, 2.0),
     'L0_attn_bv': (0.0, 0.1),
     'L0_attn_beta': (0.10000000149011612, 0.6),
     'L0_attn_ln_w': (1.0, 0.2),
     'L0_attn_ln_b': (0.0, 0.1)}
    factors = {'L0_attn_Wq': 4.618}
    for name, (base, spread) in spreads.items():
        noise = np.random.default_rng([zlib.crc32(name.encode()), seed]).standard_normal(out[name].shape)
        drawn = base * np.exp(spread * noise) if base else spread * noise
        out[name] = jnp.asarray(drawn.astype(out[name].dtype))
    for name, factor in factors.items():
        out[name] = (out[name] * factor).astype(out[name].dtype)
    return out
```

```python
from contextlib import ExitStack

import concourse.bass as bass
from concourse import mybir

F32 = mybir.dt.float32
BF16 = mybir.dt.bfloat16
I32 = mybir.dt.int32
U32 = mybir.dt.uint32
ALU = mybir.AluOpType
ACT = mybir.ActivationFunctionType
AX = mybir.AxisListType

P = 128


class GroupIndex:

    def __init__(self, number, parity, half):
        self.number, self.parity, self.half = number, parity, half

    def plus(self, k):
        return GroupIndex(self.number + k, (self.parity + k) % 2, self.half + (self.parity + k) // 2)


def due(value):
    return not isinstance(value, int) or value > 0


def spread(ap, axis, count):
    shape = list(ap.shape)
    return ap.unsqueeze(axis).broadcast_to(shape[:axis] + [count] + shape[axis:])


def decoder_layer(nc, x, ctx_in, Wh, bh, Wq, bq, Wk, bk, Wv, bv, beta, ln_w, ln_b, Wo, bo,
                  XWq, XWk, XWv, XWo, Xbo, gate_w, sh_gate, sh_up, sh_down, rt_gate, rt_up, rt_down,
                  r_scratch, routed, out):
    B, S, D = x.shape
    DE = ctx_in.shape[2]
    INNER = XWq.shape[1]
    DH = 64
    XH = INNER // DH
    AH = 16
    E, _, I = rt_gate.shape
    GB = 4
    NG = B // GB
    CH = 4
    NC = XH // CH
    EPS = 1e-5
    KVW = D + AH
    TOKENS = B * S
    ROW = 2 * D + 1
    REGION = TOKENS + P
    TILES = TOKENS // P + E
    RING = 8
    assert S == P and D == P and NG == 8 and NC == 4 and XH == 16

    ctx = ExitStack()
    with ctx:
        def sb(name, shape, dt=F32):
            return ctx.enter_context(nc.sbuf_tensor(name, shape, dt))

        def sem(name):
            return ctx.enter_context(nc.semaphore(name))

        ident = sb("ident", [P, P])
        head_mask = sb("head_mask", [P, KVW])
        neg_half = sb("neg_half", [P, GB])
        wq = sb("wq", [P, D])
        wkvh = sb("wkvh", [P, 3 * D])
        wo = sb("wo", [P, D])
        bq_col = sb("bq_col", [P, 1])
        b_hkv = sb("b_hkv", [P, 3 * D])
        beta_bc = sb("beta_bc", [P, D])
        lnw_bc = sb("lnw_bc", [P, D])
        lnb_bc = sb("lnb_bc", [P, D])
        bo_bc = sb("bo_bc", [P, D])
        xbo_bc = sb("xbo_bc", [P, D])
        A = sb("A", [P, XH, DE])
        Bw = sb("Bw", [DE, XH, D])
        xin = sb("xin", [P, 2, GB, D])
        ctx_nat = sb("ctx_nat", [P, 2, GB, DE + 1])
        ctxT = sb("ctxT", [DE + 1, 2, GB * S])
        ctxTb = sb("ctxTb", [DE, 2, GB * S], BF16)
        xn2T = sb("xn2T", [P, 2, GB * S])
        x1b = sb("x1b", [P, 2, GB, D])
        xn = sb("xn", [P, GB, D])
        xnT = sb("xnT", [P, GB * S])
        qT = sb("qT", [P, GB * S])
        hkv = sb("hkv", [P, GB, 3 * D + AH])
        kvm = sb("kvm", [P, GB, KVW])
        rden = sb("rden", [P, GB, AH])
        attn = sb("attn", [P, GB, D])
        hw = sb("hw", [P, GB, D])
        hb = sb("hb", [P, GB, D])
        gT = sb("gT", [P, GB * S])
        x1 = sb("x1", [P, GB, D])
        stats = sb("stats", [P, GB, 6])
        mv = sb("mv", [P, GB, 2])
        var_eps = sb("var_eps", [P, GB])
        rstd = sb("rstd", [P, GB])
        Y = sb("Y", [DE + 1, GB, XH, S])
        mneg = sb("mneg", [P, 2, XH])
        mrow = sb("mrow", [XH, 2, S])
        pT = sb("pT", [P, 2, XH * S])
        zs = sb("zs", [DE + 1, 2, XH * S])
        den = sb("den", [P, 2, XH])
        rrec = sb("rrec", [P, 2, XH])
        rb = sb("rb", [P, 2, XH * S])
        gate = sb("gate", [P, E])
        sh_gu = sb("sh_gu", [P, 2 * I])
        sh_dn = sb("sh_dn", [P, I // P, D])
        rt_gu = sb("rt_gu", [P, E * 2 * I])
        rt_dn = sb("rt_dn", [P, E * I // P * D])
        before = sb("before", [P, P], BF16)
        ones16 = sb("ones16", [P, P], BF16)
        expert_no = sb("expert_no", [P, E])
        next_row = sb("next_row", [P, E])
        token_no = sb("token_no", [P, 1])
        x2 = sb("x2", [P, 2, D])
        st3 = sb("st3", [P, 6])
        mv3 = sb("mv3", [P, 2])
        var3 = sb("var3", [P, 1])
        rstd3 = sb("rstd3", [P, 1])
        h3 = sb("h3", [P, 2, D])
        h3T = sb("h3T", [P, S])
        logits = sb("logits", [P, E])
        top8 = sb("top8", [P, 8])
        idx8 = sb("idx8", [P, 8], U32)
        pick = sb("pick", [P, 1])
        onehot = sb("onehot", [P, E], BF16)
        score = sb("score", [P, 2])
        tanh3 = sb("tanh3", [P, I])
        act3 = sb("act3", [P, I])
        act3T = sb("act3T", [P, I])
        rank = sb("rank", [P, E])
        row_f = sb("row_f", [P, 1])
        row_i = sb("row_i", [P, 2], I32)
        record = sb("record", [P, 2, ROW])
        blank = sb("blank", [P, ROW])
        region = sb("region", [1, E])
        steps = sb("steps", [1, E, TOKENS // P])
        upto = sb("upto", [1, E, E])
        tile_no = sb("tile_no", [1, TILES, E])
        tile_off = sb("tile_off", [1, TILES])
        cnt = sb("cnt", [1, E])
        over = sb("over", [1, E, TOKENS // P])
        ntiles = sb("ntiles", [1, E])
        part = sb("part", [1, E, E])
        tiles_to = sb("tiles_to", [1, E])
        passed = sb("passed", [1, TILES, E])
        before_t = sb("before_t", [1, TILES, E])
        t_expert = sb("t_expert", [1, TILES])
        t_first = sb("t_first", [1, TILES])
        t_row = sb("t_row", [1, TILES])
        tail_i = sb("tail_i", [1, E], I32)
        row_tab = sb("row_tab", [1, TILES], I32)
        exp_tab = sb("exp_tab", [1, TILES], I32)
        words = pT[:].rearrange("p r n -> p (r n)")
        places = [0]

        def carve(*shape):
            n = 1
            for k in shape:
                n *= k
            view = words[:, places[0]:places[0] + n]
            places[0] += n
            return view.rearrange("p (a b) -> p a b", a=shape[0])

        rec = carve(RING, ROW)
        recT = carve(2, P)
        tanh4 = carve(2, I)
        act4 = carve(2, I)
        act4T = carve(2, I)
        yo = sb("yo", [P, RING, D])

        bank = [ctx.enter_context(nc.psum_tensor(f"bank{i}", [P, 512], F32)) for i in range(8)]

        w_in = sem("s1_weights_landed")
        wx_in = sem("cross_weights_landed")
        wb_in = sem("bias_rows_landed")
        wm_in = sem("ffn_weights_landed")
        x_in = [sem("x_landed_even"), sem("x_landed_odd")]
        c_in = [sem("ctx_landed_even"), sem("ctx_landed_odd")]
        consts = sem("constants_ready")
        waited = sem("waits_that_stand_alone")
        su_pe = sem("setup_products")
        su_dve = sem("setup_copies")
        s1_pe = sem("s1_psum_ready")
        s1_act = sem("s1_act_consumed")
        s1_dve = sem("s1_dve_consumed")
        s1_stats = sem("s1_stats_ready")
        s1_rstd = sem("s1_rstd_ready")
        s1_xn = sem("s1_normalised")
        s1_ksig = sem("s1_k_sigmoid")
        s1_gate = sem("s1_gate_terms")
        s1_x1 = sem("s1_x1_ready")
        s1_x1b = sem("s1_x1b_ready")
        s1_eps = sem("s1_var_eps")
        s1_chain = sem("s1_dve_chain")
        rot_ready = sem("rot_psum_ready")
        rot_free = sem("rot_psum_consumed")
        st_ready = sem("scoresT_ready")
        exp_done = sem("exp_done")
        z_ready = sem("z_ready")
        z_evac = sem("z_copied")
        mrow_in = sem("max_row_landed")
        den_in = sem("den_landed")
        rec_done = sem("reciprocal_done")
        rscr_in = sem("reciprocal_in_dram")
        rb_in = sem("reciprocal_spread")
        norm_done = sem("z_normalised")
        s3_stats = sem("s3_stats_ready")
        s3_eps = sem("s3_var_eps")
        s3_rstd = sem("s3_rstd_ready")
        s3_h3 = sem("s3_normalised")
        s3_chain = sem("s3_dve_chain")
        s3_top = sem("s3_top_logit")
        s3_score = sem("s3_score_tanh")
        s3_tanh = sem("s3_gate_tanh")
        s3_oh = sem("s3_onehot")
        s3_st = sem("s3_bn_stats")
        routed_in = [sem("record_written_even"), sem("record_written_odd")]
        table = sem("tile_table_chain")
        blank_in = sem("blank_rows_written")
        rec_in = [sem(f"tile_landed_{r}") for r in range(RING)]
        out_in = [sem(f"tile_written_{r}") for r in range(RING)]
        ft_ready = sem("tile_turned")
        ft_copied = sem("tile_turned_copied")
        gu_ready = sem("gate_up_ready")
        gu_tanh = sem("gate_tanh")
        act_half = sem("activation_half")
        act_done = sem("activation_done")
        at_ready = sem("activation_turned")
        at_copied = sem("activation_turned_copied")
        dn_ready = sem("down_ready")
        y_done = sem("y_done")

        S1_USES = 14
        ACT_USES = [0, 5, 10, 12, 13]
        DVE_USES = [1, 2, 3, 4, 6, 7, 8, 9, 11]

        def consumed(G, u):
            if u < 0:
                G, u = G.plus(-1), u + S1_USES
            if u in ACT_USES:
                return s1_act, len(ACT_USES) * G.number + ACT_USES.index(u) + 1
            return s1_dve, len(DVE_USES) * G.number + DVE_USES.index(u) + 1

        def produced(G, u):
            return S1_USES * G.number + u + 1

        PRO_USES = XH // 2 + NC + 1
        SLOTS = B + 2

        def does(n, part):
            if not isinstance(n, int):
                return True
            lead = {"scores": 0, "max": 1, "out": -1, "ffn": -2}[part]
            return 0 <= n + lead < B

        def has_y(n, b):
            return b % 2 == 0 and (not isinstance(n, int) or n + 2 < B)

        def slot_uses(n, b):
            uses = [("stm", c) for c in range(NC)] if does(n, "max") else []
            uses += [("f", 0)] if does(n, "ffn") else []
            uses += [("mt", 0)] if does(n, "max") else []
            uses += [("f", 1), ("f", 2)] if does(n, "ffn") else []
            uses += [("y", i) for i in range(4)] if has_y(n, b) else []
            uses += [("f", 3)] if does(n, "ffn") else []
            uses += [("y", i) for i in range(4, 8)] if has_y(n, b) else []
            uses += [("f", 4), ("f", 5)] if does(n, "ffn") else []
            uses += [("out", 0)] if does(n, "out") else []
            return uses

        SLOT_OFF = [sum(len(slot_uses(None, k)) for k in range(b)) for b in range(GB)]
        PER_G = sum(len(slot_uses(None, k)) for k in range(GB))
        FIRST_G = PRO_USES + sum(len(slot_uses(n, n)) for n in range(GB))

        def base(g, b):
            if isinstance(g, int):
                return PRO_USES + sum(len(slot_uses(n, n % GB)) for n in range(GB * g + b))
            return PER_G * g + (FIRST_G - PER_G + SLOT_OFF[b])

        def use_index(G, b, kind, i=0):
            g = G.number
            n = g * GB + b
            pos = slot_uses(n if isinstance(n, int) else None, b).index((kind, i))
            even = base(g, b) if isinstance(g, int) else FIRST_G + PER_G + SLOT_OFF[b]
            return base(g, b) + pos, 2 + (even + pos) % 2

        def over_groups(engine, body):
            body(GroupIndex(0, 0, 0), GB)
            with engine.Fori(0, (NG - 4) // 2) as i:
                body(GroupIndex(i * 2 + 1, 1, i), GB)
                body(GroupIndex(i * 2 + 2, 0, i + 1), GB)
            for g in range(NG - 3, NG):
                body(GroupIndex(g, g % 2, g // 2), GB)
            body(GroupIndex(NG, NG % 2, NG // 2), SLOTS - B)

        PE_STEPS = {(2, "D"): "turn x", (3, "A"): "project first pair", (3, "C"): "project second pair",
                    (3, "D"): "project q",
                    (0, "A"): "k^T v", (0, "C"): "q k^T v", (1, "A"): "turn gated", (1, "B"): "output",
                    (2, "A"): "turn x1 and context"}
        DVE_STEPS = {(2, "A"): "stats of x", (2, "C"): "normalise x", (3, "A"): "first pair", (3, "C"): "second pair",
                     (0, "A"): "mask", (0, "D"): "attention", (0, "E"): "gating", (1, "D"): "x1",
                     (1, "E"): "normalise x1"}
        ACT_STEPS = {(2, "D"): "copy x^T", (3, "D"): "sigmoids", (1, "A"): "copy gated^T",
                     (2, "A"): "copy x1^T and context"}
        POOL_STEPS = {(2, "A"): "rstd of x", (0, "0"): "gate terms", (0, "E"): "rstd of attention",
                      (1, "E"): "rstd of x1", (2, "0"): "residual"}
        FINISHING = ("turn x1 and context", "copy x1^T and context", "residual")

        def s1_step(run, engine, steps, G, b, place):
            name = steps.get((b, place))
            ahead = 1 if b < 2 or name in FINISHING else 2
            if name is not None and not is_last(G, ahead):
                run(engine, G.plus(ahead), name)

        def prologue_steps(run, engine, steps):
            order = {(b, place): steps[b, place] for b in (2, 3, 0, 1) for place in "0ABCDE" if (b, place) in steps}
            for name in order.values():
                if name not in FINISHING:
                    run(engine, pre, name)
            for name in order.values():
                if name in FINISHING:
                    run(engine, pre, name)

        def prologue_steps_ahead(run, engine, steps):
            for b in (2, 3):
                for place in "0ABCDE":
                    name = steps.get((b, place))
                    if name is not None and name not in FINISHING:
                        run(engine, pre.plus(1), name)

        def is_last(G, k=1):
            return isinstance(G.number, int) and G.number + k > NG - 1

        def routed_before(G, b):
            return 16 * (G.number * 2 + b // 2 - 1)

        TABLE_CHAIN = 14

        def tile_runs(j, lag):
            return not isinstance(j, int) or 0 <= j - lag < TILES

        def over_tiles(engine, step):
            for j in range(RING):
                step(j, j, 0)
            with engine.Fori(1, TILES // RING) as i:
                for k in range(RING):
                    step(i * RING + k, k, i)
            for k in range(3):
                step(TILES + k, k, TILES // RING)

        pre = GroupIndex(0, 0, 0)
        CONSTS = 3 + D // AH + 19
        S3_CHAIN = 9
        CHAIN_AT = {"stats of x": 0, "attention": 1, "gating": 4, "x1": 5}
        CHAIN = 6
        rawq = pT[:, 0, 0:INNER]
        rawk = pT[0:DE, 0, INNER:2 * INNER]
        rawv = pT[0:DE, 1, 0:INNER]
        rawo = pT[:, 1, INNER:2 * INNER].rearrange("p (j n) -> p j n", n=D)
        wqT = rb[:, 0, 0:1024].rearrange("p (j n) -> p j n", n=P)
        wkT = rb[:, 0, 1024:1024 + 8 * DE].rearrange("p (j n) -> p j n", n=DE)
        wvT = rb[:, 1, 0:8 * DE].rearrange("p (j n) -> p j n", n=DE)
        NPAIR = XH // 2

        block = ctx.enter_context(nc.Block())

        def load_x(eng, G):
            if isinstance(G.number, int):
                src = x[GB * G.number:GB * G.number + GB]
            else:
                src = x[bass.ds(G.number * GB, GB)]
            eng.dma_start(xin[:, G.parity], src.rearrange("b s d -> s b d")).then_inc(x_in[G.parity], 16)

        def load_ctx(eng, G):
            if isinstance(G.number, int):
                src = ctx_in[GB * G.number:GB * G.number + GB]
            else:
                src = ctx_in[bass.ds(G.number * GB, GB)]
            eng.dma_start(ctx_nat[:, G.parity, :, 0:DE], src.rearrange("b s d -> s b d"))\
                .then_inc(c_in[G.parity], 16)

        @block.sync
        def _(sp):
            load_x(sp, pre)
            sp.dma_start(wq[:], Wq).then_inc(w_in, 16)
            sp.dma_start(wkvh[:, 0:D], Wh).then_inc(w_in, 16)
            sp.dma_start(wkvh[:, D:2 * D], Wk).then_inc(w_in, 16)
            sp.dma_start(wkvh[:, 2 * D:], Wv).then_inc(w_in, 16)
            sp.dma_start(bq_col[:], bq.rearrange("(p o) -> p o", o=1)).then_inc(w_in, 16)
            sp.dma_start(wo[:], Wo).then_inc(w_in, 16)
            sp.dma_start(rawq, XWq).then_inc(wx_in, 16)
            sp.dma_start(rawk, XWk).then_inc(wx_in, 16)
            sp.dma_start(rawv, XWv).then_inc(wx_in, 16)
            sp.dma_start(rawo, XWo.rearrange("(j p) n -> p j n", p=P)).then_inc(wx_in, 16)
            load_ctx(sp, pre)
            load_x(sp, pre.plus(1))
            load_ctx(sp, pre.plus(1))
            sp.dma_start(gate[:], gate_w).then_inc(wm_in, 16)
            sp.dma_start(sh_gu[:, 0:I], sh_gate).then_inc(wm_in, 16)
            sp.dma_start(sh_gu[:, I:], sh_up).then_inc(wm_in, 16)
            sp.dma_start(sh_dn[:], sh_down.rearrange("(k p) n -> p k n", p=P)).then_inc(wm_in, 16)
            gu_v = rt_gu[:].rearrange("p (e c) -> p e c", e=E)
            sp.dma_start(gu_v[:, :, 0:I], rt_gate.rearrange("e h i -> h e i")).then_inc(wm_in, 16)
            sp.dma_start(gu_v[:, :, I:], rt_up.rearrange("e h i -> h e i")).then_inc(wm_in, 16)
            sp.dma_start(rt_dn[:].rearrange("p (k n) -> p k n", n=D),
                         rt_down.rearrange("e (k p) n -> p (e k) n", p=P)).then_inc(wm_in, 16)
            sp.wait_ge(consts, CONSTS)
            sp.dma_start(routed[E * REGION:E * REGION + P, :], blank[:]).then_inc(blank_in, 16)

            def max_row(n, b, count):
                sp.wait_ge(rot_free, count + 1)
                sp.sem_inc(waited, 1)
                if due((n - GB + 1) * NC):
                    sp.wait_ge(st_ready, (n - GB + 1) * NC)
                    sp.sem_inc(waited, 1)
                sp.dma_start(Y[DE:DE + 1, b % GB], mrow[:, b % 2, :]).then_inc(mrow_in, 16)

            def spread_reciprocal(n, b):
                r = b % 2
                sp.wait_ge(z_evac, (n + 1) * NC)
                sp.sem_inc(waited, 1)
                sp.dma_start(den[:, r, :], zs[DE:DE + 1, r, :]).then_inc(den_in, 16)
                sp.wait_ge(rec_done, n + 1)
                sp.sem_inc(waited, 1)
                row = r_scratch[n:n + 1] if isinstance(n, int) else r_scratch[bass.ds(n, 1)]
                sp.dma_start(row.rearrange("o (p q) -> (o p) q", q=XH), rrec[:, r, :]).then_inc(rscr_in, 16)
                sp.wait_ge(rscr_in, (n + 1) * 16)
                sp.sem_inc(waited, 1)
                if due((n - 1) * NC):
                    sp.wait_ge(norm_done, (n - 1) * NC)
                    sp.sem_inc(waited, 1)
                if due(n * 16):
                    sp.wait_ge(rb_in, n * 16)
                    sp.sem_inc(waited, 1)
                sp.dma_start(rb[0:DE, r, :], row.rearrange("o f -> (o f)").partition_broadcast(DE))\
                    .then_inc(rb_in, 16)

            max_row(0, 0, PRO_USES - 1)

            def body(G, slots):
                for b in range(slots):
                    n = G.number * GB + b
                    if does(n, "max"):
                        max_row(n + 1, b + 1, use_index(G, b, "mt")[0])
                    if does(n, "scores"):
                        spread_reciprocal(n, b)
                    if b == 3 and not is_last(G, 3):
                        sp.wait_ge(s1_x1b, G.number + 2)
                        sp.sem_inc(waited, 1)
                        load_x(sp, G.plus(3))
                    if b == 3 and not is_last(G, 2):
                        load_ctx(sp, G.plus(2))

            sp.wait_ge(s1_x1b, 1)
            sp.sem_inc(waited, 1)
            load_x(sp, pre.plus(2))
            over_groups(sp, body)

            sp.wait_ge(routed_in[0], 16 * B // 2)
            sp.sem_inc(waited, 1)
            sp.wait_ge(routed_in[1], 16 * B // 2)
            sp.sem_inc(waited, 1)
            sp.wait_ge(table, TABLE_CHAIN)
            sp.sem_inc(waited, 1)
            for e in range(E):
                tail = sp.value_load(tail_i[0:1, e:e + 1], min_val=e * REGION, max_val=e * REGION + TOKENS)
                sp.dma_start(routed[bass.ds(tail, P), :], blank[:]).then_inc(blank_in, 16)
            sp.wait_ge(blank_in, 16 * (E + 1))
            sp.sem_inc(waited, 1)

            def load_tile(j, r, turn):
                if due(16 * turn):
                    sp.wait_ge(out_in[r], 16 * turn)
                    sp.sem_inc(waited, 1)
                at = row_tab[0:1, j:j + 1] if isinstance(j, int) else row_tab[0:1, bass.ds(j, 1)]
                first_row = sp.value_load(at, min_val=0, max_val=E * REGION)
                sp.dma_start(rec[:, r, :], routed[bass.ds(first_row, P), :]).then_inc(rec_in[r], 16)

            for r in range(RING):
                load_tile(r, r, 0)
            with sp.Fori(1, TILES // RING) as i:
                for r in range(RING):
                    load_tile(i * RING + r, r, i)

        def s1_rstd_pool(pool, G, k):
            pool.wait_ge(s1_stats, 3 * G.number + k + 1)
            pool.sem_inc(waited, 1)
            nc.gpsimd.tensor_scalar(var_eps[:], mv[:, :, 1], EPS, None, ALU.add).then_inc(s1_eps, 1)
            pool.wait_ge(s1_eps, 3 * G.number + k + 1)
            nc.gpsimd.tensor_tensor(rstd[:], var_eps[:], neg_half[:], ALU.pow).then_inc(s1_rstd, 1)

        def s1_pool(pool, G, step):
            if step == "rstd of x":
                s1_rstd_pool(pool, G, 0)
            if step == "gate terms":
                pool.wait_ge(s1_dve, len(DVE_USES) * G.number + 4)
                nc.gpsimd.tensor_tensor(hw[:], hkv[:, :, 0:D], spread(lnw_bc[:], 1, GB), ALU.mult)
                nc.gpsimd.tensor_tensor(hb[:], hkv[:, :, 0:D], spread(lnb_bc[:], 1, GB), ALU.mult)\
                    .then_inc(s1_gate, 1)
            if step == "rstd of attention":
                s1_rstd_pool(pool, G, 1)
            if step == "rstd of x1":
                s1_rstd_pool(pool, G, 2)
            if step == "residual":
                pool.wait_ge(s1_x1, G.number + 1)
                nc.gpsimd.tensor_tensor(x1b[:, G.parity], x1[:], spread(xbo_bc[:], 1, GB), ALU.add)\
                    .then_inc(s1_x1b, 1)

        @block.gpsimd
        def _(pool):
            bc = lambda v: v.partition_broadcast(P)
            pool.dma_start(b_hkv[:, 0:D], bc(bh)).then_inc(wb_in, 16)
            pool.dma_start(b_hkv[:, D:2 * D], bc(bk)).then_inc(wb_in, 16)
            pool.dma_start(b_hkv[:, 2 * D:], bc(bv)).then_inc(wb_in, 16)
            pool.dma_start(beta_bc[:], bc(beta)).then_inc(wb_in, 16)
            pool.dma_start(lnw_bc[:], bc(ln_w)).then_inc(wb_in, 16)
            pool.dma_start(lnb_bc[:], bc(ln_b)).then_inc(wb_in, 16)
            pool.dma_start(bo_bc[:], bc(bo)).then_inc(wb_in, 16)
            pool.dma_start(xbo_bc[:], bc(Xbo)).then_inc(wb_in, 16)
            nc.gpsimd.memset(ident[:], 0.0).then_inc(consts, 1)
            nc.gpsimd.memset(head_mask[:], 0.0).then_inc(consts, 1)
            pool.wait_ge(consts, 2)
            nc.gpsimd.affine_select(out=ident[:], in_=ident[:], compare_op=ALU.not_equal, fill=1.0, base=0,
                                    pattern=[[-1, P]], channel_multiplier=1).then_inc(consts, 1)
            hm = head_mask[:].rearrange("p (m h) -> p m h", h=AH)
            for d in range(D // AH):
                pool.wait_ge(consts, 3 + d)
                nc.gpsimd.affine_select(out=hm, in_=hm, compare_op=ALU.not_equal, fill=1.0, base=-AH * d,
                                        pattern=[[0, KVW // AH], [-1, AH]], channel_multiplier=1)\
                    .then_inc(consts, 1)
            nc.gpsimd.memset(neg_half[:], -0.5).then_inc(consts, 1)
            nc.gpsimd.memset(hkv[:, :, 3 * D:], 1.0).then_inc(consts, 1)
            nc.gpsimd.memset(ctx_nat[:, :, :, DE:DE + 1], 1.0).then_inc(consts, 1)
            pool.wait_ge(consts, 3 + D // AH + 3)
            nc.gpsimd.memset(ctxT[DE:DE + 1], 1.0).then_inc(consts, 1)
            pool.wait_ge(consts, 3 + D // AH + 4)
            nc.gpsimd.memset(before[:], 1.0).then_inc(consts, 1)
            pool.wait_ge(consts, 3 + D // AH + 5)
            nc.gpsimd.affine_select(out=before[:], in_=before[:], compare_op=ALU.is_gt, fill=0.0, base=0,
                                    pattern=[[1, P]], channel_multiplier=-1).then_inc(consts, 1)
            nc.gpsimd.memset(ones16[:], 1.0).then_inc(consts, 1)
            ramp = dict(base=0, channel_multiplier=0, allow_small_or_imprecise_dtypes=True)
            nc.gpsimd.iota(expert_no[:], [[1, E]], **ramp).then_inc(consts, 1)
            nc.gpsimd.iota(next_row[:], [[REGION, E]], **ramp).then_inc(consts, 1)
            nc.gpsimd.iota(token_no[:], [[0, 1]], base=0, channel_multiplier=1,
                           allow_small_or_imprecise_dtypes=True).then_inc(consts, 1)
            nc.gpsimd.memset(blank[:, 0:2 * D], 0.0).then_inc(consts, 1)
            nc.gpsimd.iota(blank[:, 2 * D:].bitcast(I32), [[0, 1]], base=TOKENS, channel_multiplier=1)\
                .then_inc(consts, 1)
            pool.wait_ge(consts, 3 + D // AH + 12)
            nc.gpsimd.iota(region[:], [[REGION, E]], **ramp).then_inc(consts, 1)
            pool.wait_ge(consts, 3 + D // AH + 13)
            nc.gpsimd.iota(steps[:], [[0, E], [P, TOKENS // P]], **ramp).then_inc(consts, 1)
            pool.wait_ge(consts, 3 + D // AH + 14)
            nc.gpsimd.iota(tile_no[:], [[1, TILES], [0, E]], **ramp).then_inc(consts, 1)
            pool.wait_ge(consts, 3 + D // AH + 15)
            nc.gpsimd.iota(tile_off[:], [[P, TILES]], **ramp).then_inc(consts, 1)
            pool.wait_ge(consts, 3 + D // AH + 16)
            nc.gpsimd.memset(upto[:], 1.0).then_inc(consts, 1)
            pool.wait_ge(consts, 3 + D // AH + 17)
            nc.gpsimd.affine_select(out=upto[:], in_=upto[:], compare_op=ALU.is_ge, fill=0.0, base=0,
                                    pattern=[[1, E], [-1, E]], channel_multiplier=0).then_inc(consts, 1)
            pool.wait_ge(wb_in, 16 * 8)
            nc.gpsimd.tensor_tensor(b_hkv[:, 0:D], b_hkv[:, 0:D], beta_bc[:], ALU.add).then_inc(consts, 1)
            pool.wait_ge(consts, CONSTS)
            prologue_steps(s1_pool, pool, POOL_STEPS)
            prologue_steps_ahead(s1_pool, pool, POOL_STEPS)

            def normalise(n, b, c):
                cols = slice(c * CH * S, (c + 1) * CH * S)
                if c == 0:
                    pool.wait_ge(rb_in, (n + 1) * 16)
                nc.gpsimd.tensor_tensor(zs[0:DE, b % 2, cols], zs[0:DE, b % 2, cols], rb[0:DE, b % 2, cols],
                                        ALU.mult).then_inc(norm_done, 1)

            def rstd_of_x2(m):
                pool.wait_ge(s3_stats, m + 1)
                pool.sem_inc(waited, 1)
                nc.gpsimd.tensor_scalar(var3[:], mv3[:, 1:2], EPS, None, ALU.add).then_inc(s3_eps, 1)
                pool.wait_ge(s3_eps, m + 1)
                nc.gpsimd.tensor_tensor(rstd3[:], var3[:], neg_half[:, 0:1], ALU.pow).then_inc(s3_rstd, 1)

            def scatter_records(count, r):
                pool.wait_ge(rot_free, count + 1)
                pool.sem_inc(waited, 1)
                pool.indirect_dma_start(routed, bass.IndirectOffsetOnAxis(ap=row_i[:, r:r + 1], axis=0),
                                        record[:, r, :], None).then_inc(routed_in[r], 16)

            def body(G, slots):
                for b in range(slots):
                    n = G.number * GB + b
                    s1_step(s1_pool, pool, POOL_STEPS, G, b, "0")
                    s1_step(s1_pool, pool, POOL_STEPS, G, b, "A")
                    if does(n, "out"):
                        for c in range(NC):
                            normalise(n - 1, b + 1, c)
                    s1_step(s1_pool, pool, POOL_STEPS, G, b, "E")
                    if does(n, "ffn"):
                        scatter_records(use_index(G, b, "f", 5)[0], b % 2)
                    if does(n, "out"):
                        rstd_of_x2(n - 1)

            over_groups(pool, body)

            def store_tile(j, r):
                pool.wait_ge(y_done, j + 1)
                pool.sem_inc(waited, 1)
                pool.indirect_dma_start(
                    out.rearrange("b s d -> (b s) d"),
                    bass.IndirectOffsetOnAxis(ap=rec[:, r, 2 * D:].bitcast(I32), axis=0),
                    yo[:, r, :], None, bounds_check=TOKENS - 1, oob_is_err=False).then_inc(out_in[r], 16)

            for r in range(RING):
                store_tile(r, r)
            with pool.Fori(1, TILES // RING) as i:
                for r in range(RING):
                    store_tile(i * RING + r, r)
            for r in range(RING):
                pool.wait_ge(out_in[r], 16 * (TILES // RING))

        def s1_dve_fn(dve, G, step):
            count = [CHAIN_AT.get(step, 0)]

            def link(ins):
                ins.then_inc(s1_chain, 1)
                count[0] += 1
                dve.wait_ge(s1_chain, CHAIN * G.number + count[0])
                dve.sem_inc(waited, 1)

            def emptied(u):
                dve.wait_ge(s1_pe, produced(G, u))
                return bank[u % 2]

            def stats_of(src):
                for b in range(GB):
                    last = nc.vector.bn_stats(stats[:, b, :], src[:, b, :])
                link(last)
                for b in range(GB):
                    last = nc.vector.bn_aggr(mv[:, b, :], stats[:, b, :])
                last.then_inc(s1_stats, 1)

            def normalise(dst, src, k):
                dve.wait_ge(s1_rstd, 3 * G.number + k + 1)
                for b in range(GB):
                    last = nc.vector.tensor_scalar(dst[:, b, :], src[:, b, :], mv[:, b, 0:1], rstd[:, b:b + 1],
                                                   ALU.subtract, ALU.mult)
                last.then_inc(s1_xn, 1)

            if step == "stats of x":
                dve.wait_ge(x_in[G.parity], 16 * (G.half + 1))
                stats_of(xin[:, G.parity])
            if step == "normalise x":
                normalise(xn, xin[:, G.parity], 0)
            if step in ("first pair", "second pair"):
                for u in ((1, 2) if step == "first pair" else (3, 4)):
                    ps = emptied(u)
                    if u == 1:
                        if due(G.number):
                            dve.wait_ge(s1_gate, G.number)
                    nc.vector.tensor_tensor(hkv[:, u - 1, 0:3 * D], ps[:, 0:3 * D], b_hkv[:], ALU.add)\
                        .then_inc(s1_dve, 1)
            if step == "mask":
                for u in (6, 7):
                    ps = emptied(u)
                    for j in range(2):
                        last = nc.vector.tensor_tensor(kvm[:, 2 * (u - 6) + j, :], ps[:, j * KVW:(j + 1) * KVW],
                                                       head_mask[:], ALU.mult)
                    last.then_inc(s1_dve, 1)
            if step == "attention":
                for u in (8, 9):
                    ps = emptied(u)
                    v = ps[:, 0:2 * KVW].rearrange("p (b n) -> p b n", n=KVW)
                    b0 = 2 * (u - 8)
                    link(nc.vector.reciprocal(rden[:, b0:b0 + 2, :], v[:, :, D:KVW]))
                    for j in range(2):
                        last = nc.vector.tensor_tensor(
                            attn[:, b0 + j, :].rearrange("p (m h) -> p m h", h=AH),
                            v[:, j, 0:D].rearrange("p (m h) -> p m h", h=AH),
                            spread(rden[:, b0 + j, :], 1, D // AH), ALU.mult)
                    last.then_inc(s1_dve, 1)
                dve.wait_ge(s1_dve, len(DVE_USES) * G.number + 8)
                stats_of(attn)
            if step == "gating":
                dve.wait_ge(s1_rstd, 3 * G.number + 2)
                dve.wait_ge(s1_gate, G.number + 1)
                for b in range(GB):
                    last = nc.vector.scalar_tensor_tensor(out=attn[:, b, :], in0=attn[:, b, :],
                                                          scalar=mv[:, b, 0:1], in1=hw[:, b, :],
                                                          op0=ALU.subtract, op1=ALU.mult)
                link(last)
                for b in range(GB):
                    last = nc.vector.scalar_tensor_tensor(out=attn[:, b, :], in0=attn[:, b, :],
                                                          scalar=rstd[:, b:b + 1], in1=hb[:, b, :],
                                                          op0=ALU.mult, op1=ALU.add)
                last.then_inc(s1_xn, 1)
            if step == "x1":
                ps = emptied(11)
                if due(G.number):
                    dve.wait_ge(s1_x1b, G.number)
                t = ps[:].rearrange("p (b n) -> p b n", n=D)
                nc.vector.tensor_tensor(x1[:], t, spread(bo_bc[:], 1, GB), ALU.add).then_inc(s1_dve, 1)
                dve.wait_ge(s1_dve, len(DVE_USES) * (G.number + 1))
                nc.vector.scalar_tensor_tensor(out=x1[:], in0=x1[:], scalar=0.0, in1=xin[:, G.parity],
                                               op0=ALU.max, op1=ALU.add).then_inc(s1_x1, 1)
                dve.wait_ge(s1_x1, G.number + 1)
                stats_of(x1)
            if step == "normalise x1":
                normalise(xn, x1, 2)

        @block.vector
        def _(dve):
            dve.wait_ge(consts, CONSTS)
            for k in range(2):
                dve.wait_ge(su_pe, k + 1)
                nc.vector.tensor_copy(wqT[:, 4 * k:4 * k + 4, :],
                                      bank[k][:].rearrange("p (j n) -> p j n", n=P)).then_inc(su_dve, 1)
            for w, dst in enumerate((wkT, wvT)):
                for k in range(2):
                    dve.wait_ge(su_pe, 3 + 2 * w + k)
                    nc.vector.tensor_copy(dst[:, 4 * k:4 * k + 4, :],
                                          bank[2 + 2 * w + k][:, 0:4 * DE].rearrange("p (j n) -> p j n", n=DE))\
                        .then_inc(su_dve, 1)
            for half in range(2):
                for odd in range(2):
                    dve.wait_ge(su_pe, 7 + 2 * half + odd)
                    nc.vector.tensor_copy(A[:, 8 * half + odd:8 * half + 8:2, :],
                                          bank[2 * half + odd][:, 0:4 * DE].rearrange("p (j n) -> p j n", n=DE))\
                        .then_inc(su_dve, 1)
            for half in range(2):
                for odd in range(2):
                    dve.wait_ge(su_pe, 11 + 2 * half + odd)
                    nc.vector.tensor_copy(Bw[:, 8 * half + odd:8 * half + 8:2, :],
                                          bank[4 + 2 * half + odd][0:DE, :].rearrange("p (j n) -> p j n", n=D))\
                        .then_inc(su_dve, 1)
            prologue_steps(s1_dve_fn, dve, DVE_STEPS)

            def y_out(count, bk, r0, i):
                dve.wait_ge(rot_ready, count + 1)
                src = bank[bk][0:DE, :].rearrange("p (h b t) -> p h b t", h=2, b=2)
                dst = Y[0:DE, r0:r0 + 2, 2 * i:2 * i + 2, :].rearrange("p b h t -> p h b t")
                nc.vector.tensor_copy(dst, src).then_inc(rot_free, 1)

            def head_max(count, bk, b, c):
                dve.wait_ge(rot_ready, count + 1)
                nc.vector.tensor_reduce(mneg[:, b % 2, c * CH:(c + 1) * CH],
                                        bank[bk][:].rearrange("p (h k) -> p h k", h=CH),
                                        AX.X, ALU.max, negate=True).then_inc(rot_free, 1)

            def max_copy(count, bk, n, b):
                dve.wait_ge(rot_ready, count + 1)
                if due((n - 1) * 16):
                    dve.wait_ge(mrow_in, (n - 1) * 16)
                nc.vector.tensor_copy(mrow[:, b % 2, :], bank[bk][0:XH, 0:S]).then_inc(rot_free, 1)

            for i in range(XH // 2):
                y_out(i, 2 + i % 2, 0, i)
            for c in range(NC):
                head_max(XH // 2 + c, 2 + c % 2, 0, c)
            max_copy(PRO_USES - 1, 2 + (PRO_USES - 1) % 2, 0, 0)
            prologue_steps_ahead(s1_dve_fn, dve, DVE_STEPS)

            def reciprocal(n, b):
                dve.wait_ge(den_in, (n + 1) * 16)
                if due((n - 1) * 16):
                    dve.wait_ge(rscr_in, (n - 1) * 16)
                nc.vector.reciprocal(rrec[:, b % 2, :], den[:, b % 2, :]).then_inc(rec_done, 1)

            def residual(count, bk, n, parity, b):
                dve.wait_ge(rot_ready, count + 1)
                nc.vector.tensor_tensor(x2[:, b % 2, :], bank[bk][:, 0:D], x1b[:, parity, b, :], ALU.add)\
                    .then_inc(rot_free, 1)
                dve.wait_ge(rot_free, count + 1)
                nc.vector.bn_stats(st3[:], x2[:, b % 2, :]).then_inc(s3_st, 1)
                dve.wait_ge(s3_st, n + 1)
                dve.sem_inc(waited, 1)
                nc.vector.bn_aggr(mv3[:], st3[:]).then_inc(s3_stats, 1)

            def ffn(G, b, m, step):
                r = b % 2
                done = [{"logits": 0, "gate_up": 3, "rank": 4, "scale": 7}.get(step, 0)]

                def link(ins):
                    ins.then_inc(s3_chain, 1)
                    done[0] += 1
                    dve.wait_ge(s3_chain, S3_CHAIN * m + done[0])
                    dve.sem_inc(waited, 1)

                def use(i):
                    count, bk = use_index(G, b, "f", i)
                    dve.wait_ge(rot_ready, count + 1)
                    return count, bank[bk]

                if step == "normalise":
                    dve.wait_ge(s3_rstd, m + 1)
                    nc.vector.tensor_scalar(h3[:, r, :], x2[:, r, :], mv3[:, 0:1], rstd3[:], ALU.subtract,
                                            ALU.mult).then_inc(s3_h3, 1)
                if step == "turned":
                    count, ps = use(0)
                    nc.vector.tensor_copy(h3T[:], ps[:, 0:S]).then_inc(rot_free, 1)
                if step == "logits":
                    count, ps = use(1)
                    nc.vector.tensor_copy(logits[:], ps[:, 0:E]).then_inc(rot_free, 1)
                    dve.wait_ge(rot_free, count + 1)
                    dve.sem_inc(waited, 1)
                    link(nc.vector.max(top8[:], logits[:]))
                    link(nc.vector.max_index(idx8[:], top8[:], logits[:]))
                    link(nc.vector.tensor_copy(pick[:], idx8[:, 0:1]))
                    nc.vector.tensor_scalar(onehot[:], expert_no[:], pick[:], None, ALU.is_equal)\
                        .then_inc(s3_oh, 1)
                if step == "gate_up":
                    count, ps = use(2)
                    dve.wait_ge(s3_tanh, m + 1)
                    link(nc.vector.scalar_tensor_tensor(out=act3[:], in0=tanh3[:], scalar=1.0, in1=ps[:, 0:I],
                                                        op0=ALU.add, op1=ALU.mult))
                    nc.vector.scalar_tensor_tensor(out=act3[:], in0=act3[:], scalar=0.5, in1=ps[:, I:2 * I],
                                                   op0=ALU.mult, op1=ALU.mult).then_inc(rot_free, 1)
                if step == "rank":
                    count, ps = use(3)
                    link(nc.vector.tensor_tensor(rank[:], ps[:, 0:E], next_row[:], ALU.add))
                    nc.vector.tensor_tensor(next_row[:], ps[:, E:2 * E], next_row[:], ALU.add)\
                        .then_inc(rot_free, 1)
                    link(nc.vector.tensor_tensor(rank[:], rank[:], onehot[:], ALU.mult))
                    link(nc.vector.tensor_reduce(row_f[:], rank[:], AX.X, ALU.add))
                    if due(routed_before(G, b)):
                        dve.wait_ge(routed_in[r], routed_before(G, b))
                    nc.vector.tensor_copy(row_i[:, r:r + 1], row_f[:])
                if step == "scale":
                    dve.wait_ge(s3_score, m + 1)
                    link(nc.vector.tensor_scalar(score[:, 1:2], score[:, 0:1], 0.5, 0.5, ALU.mult, ALU.add))
                    nc.vector.tensor_scalar(record[:, r, 0:D], h3[:, r, :], score[:, 1:2], None, ALU.mult)
                    link(nc.vector.tensor_copy(record[:, r, 2 * D:].bitcast(I32), token_no[:]))
                    nc.vector.tensor_scalar(token_no[:], token_no[:], float(S), None, ALU.add)
                if step == "act_turned":
                    count, ps = use(4)
                    nc.vector.tensor_copy(act3T[:], ps[:, 0:I]).then_inc(rot_free, 1)
                if step == "shared":
                    count, ps = use(5)
                    nc.vector.tensor_tensor(record[:, r, D:2 * D], ps[:, 0:D], x2[:, r, :], ALU.add)\
                        .then_inc(rot_free, 1)

            def body(G, slots):
                for b in range(slots):
                    n = G.number * GB + b
                    m = n - 2
                    f = (lambda step: ffn(G, b, m, step)) if does(n, "ffn") else (lambda step: None)
                    s1 = lambda place: s1_step(s1_dve_fn, dve, DVE_STEPS, G, b, place)

                    def y(i):
                        if has_y(n, b):
                            for k in range(i, i + 4):
                                y_out(*use_index(G, b, "y", k), (b + 2) % GB, k)

                    if does(n, "max"):
                        for c in range(NC):
                            head_max(*use_index(G, b, "stm", c), b + 1, c)
                    f("normalise")
                    f("turned")
                    if does(n, "max"):
                        max_copy(*use_index(G, b, "mt"), n + 1, b + 1)
                    if does(n, "out"):
                        reciprocal(n - 1, b + 1)
                    f("logits")
                    s1("A")
                    f("gate_up")
                    y(0)
                    f("rank")
                    f("scale")
                    s1("C")
                    y(4)
                    f("act_turned")
                    s1("D")
                    f("shared")
                    s1("E")
                    if does(n, "out"):
                        residual(*use_index(G, b, "out"), n - 1, G.parity if b else 1 - G.parity, (b - 1) % GB)

            over_groups(dve, body)

            chain = [0]

            def link(ins):
                ins.then_inc(table, 1)
                chain[0] += 1
                dve.wait_ge(table, chain[0])

            link(nc.vector.tensor_tensor(cnt[:], next_row[0:1, :], region[:], ALU.subtract))
            link(nc.vector.tensor_copy(tail_i[:], next_row[0:1, :]))
            link(nc.vector.tensor_tensor(over[:], spread(cnt[:], 2, TOKENS // P), steps[:], ALU.is_gt))
            link(nc.vector.tensor_reduce(ntiles[:], over[:], AX.X, ALU.add))
            link(nc.vector.tensor_tensor(part[:], spread(ntiles[:], 1, E), upto[:], ALU.mult))
            link(nc.vector.tensor_reduce(tiles_to[:], part[:], AX.X, ALU.add))
            link(nc.vector.tensor_tensor(passed[:], spread(tiles_to[:], 1, TILES), tile_no[:], ALU.is_le))
            link(nc.vector.tensor_reduce(t_expert[:], passed[:], AX.X, ALU.add))
            link(nc.vector.tensor_tensor(before_t[:], passed[:], spread(ntiles[:], 1, TILES), ALU.mult))
            link(nc.vector.tensor_reduce(t_first[:], before_t[:], AX.X, ALU.add))
            link(nc.vector.scalar_tensor_tensor(out=t_row[:], in0=t_first[:], scalar=-float(P), in1=tile_off[:],
                                                op0=ALU.mult, op1=ALU.add))
            link(nc.vector.scalar_tensor_tensor(out=t_row[:], in0=t_expert[:], scalar=float(REGION),
                                                in1=t_row[:], op0=ALU.mult, op1=ALU.add))
            link(nc.vector.tensor_scalar(row_tab[:], t_row[:], float(E * REGION), None, ALU.min))
            link(nc.vector.tensor_scalar(exp_tab[:], t_expert[:], float(E - 1), None, ALU.min))
            assert chain[0] == TABLE_CHAIN

            def activate(j, r2):
                dve.wait_ge(gu_tanh, j + 1)
                ps = bank[2 + r2]
                if due(j - 1):
                    dve.wait_ge(at_ready, j - 1)
                nc.vector.scalar_tensor_tensor(out=act4[:, r2], in0=tanh4[:, r2], scalar=1.0, in1=ps[:, 0:I],
                                               op0=ALU.add, op1=ALU.mult).then_inc(act_half, 1)
                dve.wait_ge(act_half, j + 1)
                nc.vector.scalar_tensor_tensor(out=act4[:, r2], in0=act4[:, r2], scalar=0.5,
                                               in1=ps[:, I:2 * I], op0=ALU.mult, op1=ALU.mult)\
                    .then_inc(act_done, 1)

            def finish(j, r, r2, turn):
                dve.wait_ge(dn_ready, j + 1)
                if due(16 * turn):
                    dve.wait_ge(out_in[r], 16 * turn)
                nc.vector.tensor_tensor(yo[:, r, :], bank[6 + r2][:, 0:D], rec[:, r, D:2 * D], ALU.add)\
                    .then_inc(y_done, 1)

            def step(j, k, turn):
                if tile_runs(j, 1):
                    activate(j - 1, (k - 1) % 2)
                if tile_runs(j, 3):
                    finish(j - 3, (k - 3) % RING, (k - 3) % 2, turn - (1 if k < 3 else 0))

            over_tiles(dve, step)

        def s1_act_fn(act, G, step):
            if step == "copy x^T":
                act.wait_ge(s1_pe, produced(G, 0))
                nc.scalar.copy(xnT[:], bank[0][:]).then_inc(s1_act, 1)
            if step == "sigmoids":
                act.wait_ge(s1_pe, produced(G, 5))
                nc.scalar.activation(qT[:], bank[1][:], ACT.Sigmoid, bias=bq_col[:]).then_inc(s1_act, 1)
                act.wait_ge(s1_dve, len(DVE_USES) * G.number + 4)
                nc.scalar.activation(hkv[:, :, D:2 * D], hkv[:, :, D:2 * D], ACT.Sigmoid).then_inc(s1_ksig, 1)
            if step == "copy gated^T":
                act.wait_ge(s1_pe, produced(G, 10))
                nc.scalar.copy(gT[:], bank[0][:]).then_inc(s1_act, 1)
            if step == "copy x1^T and context":
                act.wait_ge(s1_pe, produced(G, 12))
                nc.scalar.copy(xn2T[:, G.parity], bank[0][:]).then_inc(s1_act, 1)
                act.wait_ge(s1_pe, produced(G, 13))
                nc.scalar.copy(ctxTb[:, G.parity], bank[1][0:DE, :])
                nc.scalar.copy(ctxT[0:DE, G.parity], bank[1][0:DE, :]).then_inc(s1_act, 1)

        @block.scalar
        def _(act):
            act.wait_ge(consts, CONSTS)
            act.wait_ge(w_in, 16 * 6)
            prologue_steps(s1_act_fn, act, ACT_STEPS)
            prologue_steps_ahead(s1_act_fn, act, ACT_STEPS)

            def exp_chunk(n, b, c):
                q = n * NC + c
                act.wait_ge(st_ready, q + 1)
                if due(q - 2 * NC + 1):
                    act.wait_ge(z_ready, q - 2 * NC + 1)
                nc.scalar.activation(pT[:, b % 2, c * CH * S:(c + 1) * CH * S], bank[4 + c % 2][:], ACT.Exp,
                                     scale=float(DH) ** -0.5).then_inc(exp_done, 1)

            def z_copy(G, n, b, c):
                act.wait_ge(z_ready, n * NC + c + 1)
                if c == 0:
                    act.wait_ge(rot_ready, base(G.number, b))
                nc.scalar.copy(zs[:, b % 2, c * CH * S:(c + 1) * CH * S], bank[6 + c % 2][0:DE + 1, :])\
                    .then_inc(z_evac, 1)

            def score_tanh(m):
                act.wait_ge(s3_chain, S3_CHAIN * m + 1)
                nc.scalar.activation(score[:, 0:1], top8[:, 0:1], ACT.Tanh, scale=0.5).then_inc(s3_score, 1)

            def gate_tanh(count, bk):
                act.wait_ge(rot_ready, count + 1)
                nc.scalar.activation(tanh3[:], bank[bk][:, 0:I], ACT.Tanh, scale=0.5).then_inc(s3_tanh, 1)

            def body(G, slots):
                for b in range(slots):
                    n = G.number * GB + b
                    z = (lambda c: z_copy(G, n, b, c)) if does(n, "scores") else (lambda c: None)
                    e = (lambda c: exp_chunk(n, b, c)) if does(n, "scores") else (lambda c: None)
                    s1 = lambda place: s1_step(s1_act_fn, act, ACT_STEPS, G, b, place)
                    e(0)
                    e(1)
                    z(0)
                    s1("A")
                    e(2)
                    if does(n, "ffn"):
                        gate_tanh(*use_index(G, b, "f", 2))
                    z(1)
                    e(3)
                    if does(n, "ffn"):
                        score_tanh(n - 2)
                    z(2)
                    z(3)
                    s1("D")

            over_groups(act, body)

            def step(j, k, turn):
                if tile_runs(j, 0):
                    act.wait_ge(ft_ready, j + 1)
                    nc.scalar.copy(recT[:, k % 2], bank[k % 2][:, 0:P]).then_inc(ft_copied, 1)
                if tile_runs(j, 1):
                    act.wait_ge(gu_ready, j)
                    if due(j - 2):
                        act.wait_ge(act_done, j - 2)
                    nc.scalar.activation(tanh4[:, (k - 1) % 2], bank[2 + (k - 1) % 2][:, 0:I], ACT.Tanh,
                                         scale=0.5).then_inc(gu_tanh, 1)
                if tile_runs(j, 2):
                    act.wait_ge(at_ready, j - 1)
                    if due(j - 3):
                        act.wait_ge(dn_ready, j - 3)
                    nc.scalar.copy(act4T[:, k % 2], bank[4 + k % 2][:, 0:I]).then_inc(at_copied, 1)

            over_tiles(act, step)

        def s1_pe_fn(pe, G, step):
            def free(u):
                if due(consumed(G, u - 2)[1]):
                    pe.wait_ge(*consumed(G, u - 2))
                return bank[u % 2]

            def turned(u, src, rows, wide=D):
                ps = free(u)
                for b in range(GB):
                    last = pe.transpose(ps[0:wide, b * S:(b + 1) * S], src[:, b, 0:wide], ident[:])
                last.then_inc(s1_pe, 1)

            def project(u):
                ps = free(u)
                b = u - 1
                pe.matmul(ps[:, 0:3 * D], xnT[:, b * S:(b + 1) * S], wkvh[:], start=True, stop=True)\
                    .then_inc(s1_pe, 1)

            if step == "turn x":
                pe.wait_ge(s1_xn, 3 * G.number + 1)
                turned(0, xn, D)
            if step == "project first pair":
                pe.wait_ge(*consumed(G, 0))
                project(1)
                project(2)
            if step == "project second pair":
                project(3)
                project(4)
            if step == "project q":
                pe.matmul(free(5)[:], wq[:], xnT[:], start=True, stop=True).then_inc(s1_pe, 1)
            if step == "k^T v":
                pe.wait_ge(s1_ksig, G.number + 1)
                for u in (6, 7):
                    ps = free(u)
                    for j in range(2):
                        b = 2 * (u - 6) + j
                        last = pe.matmul(ps[:, j * KVW:(j + 1) * KVW], hkv[:, b, D:2 * D], hkv[:, b, 2 * D:],
                                         start=True, stop=True)
                    last.then_inc(s1_pe, 1)
            if step == "q k^T v":
                for u in (8, 9):
                    ps = free(u)
                    pe.wait_ge(*consumed(G, u - 2))
                    for j in range(2):
                        b = 2 * (u - 8) + j
                        last = pe.matmul(ps[:, j * KVW:(j + 1) * KVW], qT[:, b * S:(b + 1) * S], kvm[:, b, :],
                                         start=True, stop=True)
                    last.then_inc(s1_pe, 1)
            if step == "turn gated":
                pe.wait_ge(s1_xn, 3 * G.number + 2)
                turned(10, attn, D)
            if step == "output":
                ps = free(11)
                pe.wait_ge(*consumed(G, 10))
                for b in range(GB):
                    last = pe.matmul(ps[:, b * D:(b + 1) * D], gT[:, b * S:(b + 1) * S], wo[:],
                                     start=True, stop=True)
                last.then_inc(s1_pe, 1)
            if step == "turn x1 and context":
                pe.wait_ge(s1_xn, 3 * G.number + 3)
                turned(12, xn, D)
                pe.wait_ge(c_in[G.parity], 16 * (G.half + 1))
                turned(13, ctx_nat[:, G.parity], DE, DE)

        @block.tensor
        def _(pe):
            pe.wait_ge(consts, CONSTS)
            pe.wait_ge(w_in, 16 * 6)
            pe.wait_ge(wx_in, 16 * 4)
            for k in range(2):
                for j in range(4):
                    last = pe.transpose(bank[k][:, j * P:(j + 1) * P],
                                        rawq[:, (4 * k + j) * P:(4 * k + j + 1) * P], ident[:])
                last.then_inc(su_pe, 1)
            for w, src in enumerate((rawk, rawv)):
                for k in range(2):
                    for j in range(4):
                        last = pe.transpose(bank[2 + 2 * w + k][:, j * DE:(j + 1) * DE],
                                            src[:, (4 * k + j) * P:(4 * k + j + 1) * P], ident[0:DE, 0:DE])
                    last.then_inc(su_pe, 1)
            pe.wait_ge(su_dve, 6)
            for half in range(2):
                for odd in range(2):
                    rows = slice(DH * odd, DH * odd + DH)
                    for j in range(4):
                        last = pe.matmul(bank[2 * half + odd][:, j * DE:(j + 1) * DE],
                                         wqT[rows, 4 * half + j, :], wkT[rows, 4 * half + j, :],
                                         start=True, stop=True)
                    last.then_inc(su_pe, 1)
            for half in range(2):
                for odd in range(2):
                    rows = slice(DH * odd, DH * odd + DH)
                    for j in range(4):
                        last = pe.matmul(bank[4 + 2 * half + odd][0:DE, j * D:(j + 1) * D],
                                         wvT[rows, 4 * half + j, :], rawo[rows, 4 * half + j, :],
                                         start=True, stop=True)
                    last.then_inc(su_pe, 1)
            pe.wait_ge(su_dve, 14)
            prologue_steps(s1_pe_fn, pe, PE_STEPS)

            def y_product(count, bk, G, half, i):
                if due(count - 1):
                    pe.wait_ge(rot_free, count - 1)
                for j in range(2):
                    last = pe.matmul(bank[bk][0:DE, j * 256:(j + 1) * 256], A[:, 2 * i + j, :],
                                     xn2T[:, G.parity, half * 256:(half + 1) * 256], start=True, stop=True)
                last.then_inc(rot_ready, 1)

            def score_rows(count, bk, parity, b, c):
                pe.wait_ge(rot_free, count - 1)
                for j in range(CH):
                    h = c * CH + j
                    y16 = Y[0:DE, b % GB, h, :].bitcast(BF16)[:, 1::2]
                    last = pe.matmul(bank[bk][:, j * S:(j + 1) * S], y16,
                                     ctxTb[:, parity, (b % GB) * S:(b % GB + 1) * S], start=True, stop=True)
                last.then_inc(rot_ready, 1)

            def max_turn(count, bk, last_chunk, b):
                pe.wait_ge(rot_free, last_chunk + 1)
                pe.wait_ge(rot_free, count - 1)
                pe.transpose(bank[bk][0:XH, 0:S], mneg[:, b % 2, :], ident[:]).then_inc(rot_ready, 1)

            for i in range(XH // 2):
                if i == 0:
                    pe.wait_ge(s1_act, len(ACT_USES))
                y_product(i, 2 + i % 2, pre, 0, i)
            pe.wait_ge(rot_free, XH // 2)
            for c in range(NC):
                score_rows(XH // 2 + c, 2 + c % 2, 0, 0, c)
            max_turn(PRO_USES - 1, 2 + (PRO_USES - 1) % 2, PRO_USES - 2, 0)
            prologue_steps_ahead(s1_pe_fn, pe, PE_STEPS)

            def scores_T(G, n, b, c):
                q = n * NC + c
                if c == 0:
                    pe.wait_ge(mrow_in, (n + 1) * 16)
                if due(q - 1):
                    pe.wait_ge(exp_done, q - 1)
                pe.matmul(bank[4 + c % 2][:], ctxT[:, G.parity, b * S:(b + 1) * S],
                          Y[:, b, c * CH:(c + 1) * CH, :], start=True, stop=True).then_inc(st_ready, 1)

            def z_product(G, n, b, c):
                q = n * NC + c
                pe.wait_ge(exp_done, q + 1)
                if due(q - 1):
                    pe.wait_ge(z_evac, q - 1)
                pe.matmul(bank[6 + c % 2][0:DE + 1, :], ctx_nat[:, G.parity, b, :],
                          pT[:, b % 2, c * CH * S:(c + 1) * CH * S], start=True, stop=True).then_inc(z_ready, 1)

            def out_product(count, bk, n, b):
                pe.wait_ge(rot_free, count - 1)
                for h in range(XH):
                    if h % CH == 0:
                        pe.wait_ge(norm_done, n * NC + h // CH + 1)
                    last = pe.matmul(bank[bk][:, 0:D], zs[0:DE, b % 2, h * S:(h + 1) * S], Bw[:, h, :],
                                     start=(h == 0), stop=(h == XH - 1))
                last.then_inc(rot_ready, 1)

            def ffn(G, b, m, i):
                r = b % 2
                count, bk = use_index(G, b, "f", i)
                ps = bank[bk]
                pe.wait_ge(rot_free, count - 1)
                if i == 0:
                    pe.wait_ge(s3_h3, m + 1)
                    last = pe.transpose(ps[:, 0:S], h3[:, r, :], ident[:])
                if i == 1:
                    pe.wait_ge(rot_free, use_index(G, b, "f", 0)[0] + 1)
                    last = pe.matmul(ps[:, 0:E], h3T[:], gate[:], start=True, stop=True)
                if i == 2:
                    last = pe.matmul(ps[:], h3T[:], sh_gu[:], start=True, stop=True)
                if i == 3:
                    pe.wait_ge(s3_oh, m + 1)
                    pe.matmul(ps[:, 0:E], before[:], onehot[:], start=True, stop=True)
                    last = pe.matmul(ps[:, E:2 * E], ones16[:], onehot[:], start=True, stop=True)
                if i == 4:
                    pe.wait_ge(rot_free, use_index(G, b, "f", 2)[0] + 1)
                    for k in range(I // P):
                        last = pe.transpose(ps[:, k * P:(k + 1) * P], act3[:, k * P:(k + 1) * P], ident[:])
                if i == 5:
                    pe.wait_ge(rot_free, use_index(G, b, "f", 4)[0] + 1)
                    for k in range(I // P):
                        last = pe.matmul(ps[:, 0:D], act3T[:, k * P:(k + 1) * P], sh_dn[:, k, :],
                                         start=(k == 0), stop=(k == I // P - 1))
                last.then_inc(rot_ready, 1)

            def body(G, slots):
                def y(n, b, i):
                    if has_y(n, b):
                        source = G if b == 0 else G.plus(1)
                        if i == 0:
                            pe.wait_ge(s1_act, len(ACT_USES) * (source.number + 1))
                        for k in range(i, i + 4):
                            y_product(*use_index(G, b, "y", k), source, 1 if b == 0 else 0, k)

                for b in range(slots):
                    n = G.number * GB + b
                    f = (lambda i: ffn(G, b, n - 2, i)) if does(n, "ffn") else (lambda i: None)
                    st = (lambda c: scores_T(G, n, b, c)) if does(n, "scores") else (lambda c: None)
                    z = (lambda c: z_product(G, n, b, c)) if does(n, "scores") else (lambda c: None)
                    s1 = lambda place: s1_step(s1_pe_fn, pe, PE_STEPS, G, b, place)

                    def rows(c):
                        if does(n, "max"):
                            if c == 0:
                                pe.wait_ge(rot_free, base(G.number, b))
                            score_rows(*use_index(G, b, "stm", c), (G.parity + (b == 3)) % 2, b + 1, c)

                    st(0)
                    rows(0)
                    rows(1)
                    st(1)
                    rows(2)
                    rows(3)
                    z(0)
                    s1("A")
                    f(0)
                    st(2)
                    if does(n, "max"):
                        max_turn(*use_index(G, b, "mt"), use_index(G, b, "stm", NC - 1)[0], b + 1)
                    f(1)
                    f(2)
                    z(1)
                    s1("B")
                    y(n, b, 0)
                    st(3)
                    f(3)
                    z(2)
                    s1("C")
                    y(n, b, 4)
                    f(4)
                    z(3)
                    s1("D")
                    f(5)
                    if does(n, "out"):
                        out_product(*use_index(G, b, "out"), n - 1, b + 1)

            over_groups(pe, body)

            pe.wait_ge(table, TABLE_CHAIN)
            pe.wait_ge(rot_free, base(NG, SLOTS - B))

            def expert_of(j):
                at = exp_tab[0:1, j:j + 1] if isinstance(j, int) else exp_tab[0:1, bass.ds(j, 1)]
                return pe.value_load(at, min_val=0, max_val=E - 1)

            def step(j, k, turn):
                if tile_runs(j, 0):
                    r = k % RING
                    pe.wait_ge(rec_in[r], 16 * (turn + 1))
                    if due(j - 1):
                        pe.wait_ge(ft_copied, j - 1)
                    pe.transpose(bank[k % 2][:, 0:P], rec[:, r, 0:D], ident[:]).then_inc(ft_ready, 1)
                if tile_runs(j, 1):
                    e = expert_of(j - 1)
                    pe.wait_ge(ft_copied, j)
                    if due(j - 2):
                        pe.wait_ge(act_done, j - 2)
                    pe.matmul(bank[2 + (k - 1) % 2][:], recT[:, (k - 1) % 2], rt_gu[:, bass.ds(e * (2 * I), 2 * I)],
                              start=True, stop=True).then_inc(gu_ready, 1)
                if tile_runs(j, 2):
                    pe.wait_ge(act_done, j - 1)
                    if due(j - 3):
                        pe.wait_ge(at_copied, j - 3)
                    for h in range(I // P):
                        last = pe.transpose(bank[4 + k % 2][:, h * P:(h + 1) * P],
                                            act4[:, k % 2, h * P:(h + 1) * P], ident[:])
                    last.then_inc(at_ready, 1)
                if tile_runs(j, 3):
                    e = expert_of(j - 3)
                    pe.wait_ge(at_copied, j - 2)
                    if due(j - 4):
                        pe.wait_ge(y_done, j - 4)
                    for h in range(I // P):
                        last = pe.matmul(bank[6 + (k - 3) % 2][:, 0:D], act4T[:, (k - 3) % 2, h * P:(h + 1) * P],
                                         rt_dn[:, bass.ds(e * I + h * P, P)], start=(h == 0),
                                         stop=(h == I // P - 1))
                    last.then_inc(dn_ready, 1)

            pe.wait_ge(wm_in, 16 * 7)
            over_tiles(pe, step)


_INS = ['x', 'ctx_768', 'L0_attn_Wh', 'L0_attn_bh', 'L0_attn_Wq', 'L0_attn_bq', 'L0_attn_Wk', 'L0_attn_bk',
        'L0_attn_Wv', 'L0_attn_bv', 'L0_attn_beta', 'L0_attn_ln_w', 'L0_attn_ln_b', 'L0_attn_Wo', 'L0_attn_bo',
        'L0_xattn_Wq', 'L0_xattn_Wk', 'L0_xattn_Wv', 'L0_xattn_Wo', 'L0_xattn_bo', 'L0_ffn_gate_w',
        'L0_ffn_sh_gate', 'L0_ffn_sh_up', 'L0_ffn_sh_down', 'L0_ffn_rt_gate', 'L0_ffn_rt_up', 'L0_ffn_rt_down']


def kernel(**inputs):
    import numpy as _np
    import concourse.bacc as _bacc
    from concourse import mybir as _mybir
    from concourse.bass_utils import run_bass_kernel_spmd as _run

    nc = _bacc.Bacc("TRN2", target_bir_lowering=False, num_devices=1)
    arrays, args = {}, []
    for name in _INS:
        a = _np.ascontiguousarray(inputs[name])
        arrays[f"in_{name}_dram"] = a
        args.append(nc.dram_tensor(f"in_{name}_dram", a.shape, _mybir.dt.from_np(a.dtype), kind="ExternalInput").ap())
    batch, tokens, width = inputs['x'].shape
    experts = inputs['L0_ffn_gate_w'].shape[1]
    heads = inputs['L0_xattn_Wq'].shape[1] // 64
    f32 = _mybir.dt.float32
    r_scratch = nc.dram_tensor("r_scratch", (batch, heads * tokens), f32, kind="Internal").ap()
    routed = nc.dram_tensor("routed", (experts * (batch * tokens + 128) + 128, 2 * width + 1), f32,
                            kind="Internal").ap()
    out = nc.dram_tensor("out_0_dram", (batch, tokens, width), f32, kind="ExternalOutput").ap()
    decoder_layer(nc, *args, r_scratch, routed, out)
    r = _run(nc, [arrays], core_ids=[0])
    return r.results[0]["out_0_dram"]
```

```python
from contextlib import ExitStack

import concourse.bass as bass
from concourse import mybir

F32 = mybir.dt.float32
F32R = mybir.dt.float32r
BF16 = mybir.dt.bfloat16
I32 = mybir.dt.int32
U32 = mybir.dt.uint32
ALU = mybir.AluOpType
ACT = mybir.ActivationFunctionType
AX = mybir.AxisListType

P = 128


class GroupIndex:

    def __init__(self, number, parity, half):
        self.number, self.parity, self.half = number, parity, half

    def plus(self, k):
        return GroupIndex(self.number + k, (self.parity + k) % 2, self.half + (self.parity + k) // 2)


def due(value):
    return not isinstance(value, int) or value > 0


def by_register(value):
    return not isinstance(value, int)


def spread(ap, axis, count):
    shape = list(ap.shape)
    return ap.unsqueeze(axis).broadcast_to(shape[:axis] + [count] + shape[axis:])


def decoder_layer(nc, x, ctx_in, Wh, bh, Wq, bq, Wk, bk, Wv, bv, beta, ln_w, ln_b, Wo, bo,
                  XWq, XWk, XWv, XWo, Xbo, gate_w, sh_gate, sh_up, sh_down, rt_gate, rt_up, rt_down,
                  r_scratch, routed, out):
    B, S, D = x.shape
    DE = ctx_in.shape[2]
    INNER = XWq.shape[1]
    DH = 64
    XH = INNER // DH
    AH = 16
    E, _, I = rt_gate.shape
    GB = 4
    NG = B // GB
    CH = 4
    NC = XH // CH
    EPS = 1e-5
    KVW = D + AH
    TOKENS = B * S
    ROW = 2 * D + 1
    REGION = TOKENS + P
    TILES = TOKENS // P + E
    RING = 8
    assert S == P and D == P and NG == 8 and NC == 4 and XH == 16

    ctx = ExitStack()
    with ctx:
        def sb(name, shape, dt=F32):
            return ctx.enter_context(nc.sbuf_tensor(name, shape, dt))

        def sem(name):
            return ctx.enter_context(nc.semaphore(name))

        ident = sb("ident", [P, P])
        head_mask = sb("head_mask", [P, KVW])
        neg_half = sb("neg_half", [P, GB])
        wq = sb("wq", [P, D])
        wkvh = sb("wkvh", [P, 3 * D])
        wo = sb("wo", [P, D])
        bq_col = sb("bq_col", [P, 1])
        b_hkv = sb("b_hkv", [P, 3 * D])
        beta_bc = sb("beta_bc", [P, D])
        lnw_bc = sb("lnw_bc", [P, D])
        lnb_bc = sb("lnb_bc", [P, D])
        bo_bc = sb("bo_bc", [P, D])
        xbo_bc = sb("xbo_bc", [P, D])
        A_hi = sb("A_hi", [P, XH, DE], F32R)
        A_lo = sb("A_lo", [P, XH, DE], F32R)
        Bw = sb("Bw", [DE, XH, D])
        xin = sb("xin", [P, 2, GB, D])
        ctx_nat = sb("ctx_nat", [P, 2, GB, DE + 1])
        ctxT = sb("ctxT", [DE + 1, 2, GB * S])
        ctxTb = sb("ctxTb", [DE, 2, GB * S], BF16)
        xn2T_hi = sb("xn2T_hi", [P, 2, GB * S], F32R)
        xn2T_lo = sb("xn2T_lo", [P, 2, GB * S], F32R)
        x1b = sb("x1b", [P, 2, GB, D])
        xn = sb("xn", [P, GB, D])
        xnT = sb("xnT", [P, GB * S])
        qT = sb("qT", [P, GB * S])
        hkv = sb("hkv", [P, GB, 3 * D + AH])
        kvm = sb("kvm", [P, GB, KVW])
        rden = sb("rden", [P, GB, AH])
        attn = sb("attn", [P, GB, D])
        hw = sb("hw", [P, GB, D])
        hb = sb("hb", [P, GB, D])
        gT = sb("gT", [P, GB * S])
        x1 = sb("x1", [P, GB, D])
        stats = sb("stats", [P, GB, 6])
        mv = sb("mv", [P, GB, 2])
        var_eps = sb("var_eps", [P, GB])
        rstd = sb("rstd", [P, GB])
        Y = sb("Y", [DE + 1, GB, XH, S])
        mneg = sb("mneg", [P, 2, XH])
        mrow = sb("mrow", [XH, 2, S])
        pT = sb("pT", [P, 2, XH * S])
        zs = sb("zs", [DE + 1, 2, XH * S])
        den = sb("den", [P, 2, XH])
        rrec = sb("rrec", [P, 2, XH])
        rb = sb("rb", [P, 2, XH * S])
        gate = sb("gate", [P, E])
        sh_gu = sb("sh_gu", [P, 2 * I])
        sh_dn = sb("sh_dn", [P, I // P, D])
        rt_gu = sb("rt_gu", [P, E * 2 * I])
        rt_dn = sb("rt_dn", [P, E * I // P * D])
        before = sb("before", [P, P], BF16)
        ones16 = sb("ones16", [P, P], BF16)
        expert_no = sb("expert_no", [P, E])
        next_row = sb("next_row", [P, E])
        token_no = sb("token_no", [P, 1])
        x2 = sb("x2", [P, 2, D])
        st3 = sb("st3", [P, 6])
        mv3 = sb("mv3", [P, 2])
        var3 = sb("var3", [P, 1])
        rstd3 = sb("rstd3", [P, 1])
        h3 = sb("h3", [P, 2, D])
        h3T = sb("h3T", [P, S])
        logits = sb("logits", [P, E])
        top8 = sb("top8", [P, 8])
        idx8 = sb("idx8", [P, 8], U32)
        pick = sb("pick", [P, 1])
        onehot = sb("onehot", [P, E], BF16)
        score = sb("score", [P, 2])
        tanh3 = sb("tanh3", [P, I])
        act3 = sb("act3", [P, I])
        act3T = sb("act3T", [P, I])
        rank = sb("rank", [P, E])
        row_f = sb("row_f", [P, 1])
        row_i = sb("row_i", [P, 2], I32)
        record = sb("record", [P, 2, ROW])
        blank = sb("blank", [P, ROW])
        region = sb("region", [1, E])
        steps = sb("steps", [1, E, TOKENS // P])
        upto = sb("upto", [1, E, E])
        tile_no = sb("tile_no", [1, TILES, E])
        tile_off = sb("tile_off", [1, TILES])
        cnt = sb("cnt", [1, E])
        over = sb("over", [1, E, TOKENS // P])
        ntiles = sb("ntiles", [1, E])
        part = sb("part", [1, E, E])
        tiles_to = sb("tiles_to", [1, E])
        passed = sb("passed", [1, TILES, E])
        before_t = sb("before_t", [1, TILES, E])
        t_expert = sb("t_expert", [1, TILES])
        t_first = sb("t_first", [1, TILES])
        t_row = sb("t_row", [1, TILES])
        tail_i = sb("tail_i", [1, E], I32)
        row_tab = sb("row_tab", [1, TILES], I32)
        exp_tab = sb("exp_tab", [1, TILES], I32)
        words = pT[:].rearrange("p r n -> p (r n)")
        places = [0]

        def carve(*shape):
            n = 1
            for k in shape:
                n *= k
            view = words[:, places[0]:places[0] + n]
            places[0] += n
            return view.rearrange("p (a b) -> p a b", a=shape[0])

        rec = carve(RING, ROW)
        recT = carve(2, P)
        tanh4 = carve(2, I)
        act4 = carve(2, I)
        act4T = carve(2, I)
        yo = sb("yo", [P, RING, D])

        bank = [ctx.enter_context(nc.psum_tensor(f"bank{i}", [P, 512], F32)) for i in range(8)]

        w_in = sem("s1_weights_landed")
        wx_in = sem("cross_weights_landed")
        wo_in = sem("output_weights_landed")
        wb_in = sem("bias_rows_landed")
        wl_in = sem("norm_and_output_rows_landed")
        wm_in = sem("ffn_weights_landed")
        x_in = [sem("x_landed_even"), sem("x_landed_odd")]
        c_in = [sem("ctx_landed_even"), sem("ctx_landed_odd")]
        consts = sem("constants_ready")
        waited = sem("waits_that_stand_alone")
        su_pe = sem("setup_products")
        su_dve = sem("setup_copies_dve")
        su_act = sem("setup_copies_act")
        s1_pe = sem("s1_psum_ready")
        s1_act = sem("s1_act_consumed")
        s1_dve = sem("s1_dve_consumed")
        s1_stats = sem("s1_stats_ready")
        s1_rstd = sem("s1_rstd_ready")
        s1_xn = sem("s1_normalised")
        s1_ksig = sem("s1_k_sigmoid")
        s1_hi = sem("s1_x1T_high_part")
        s1_gate = sem("s1_gate_terms")
        s1_x1 = sem("s1_x1_ready")
        s1_x1b = sem("s1_x1b_ready")
        s1_eps = sem("s1_var_eps")
        s1_chain = sem("s1_dve_chain")
        rot_ready = sem("rot_psum_ready")
        rot_free = sem("rot_psum_consumed")
        st_ready = sem("scoresT_ready")
        exp_done = sem("exp_done")
        z_ready = sem("z_ready")
        z_evac = sem("z_copied")
        mrow_in = sem("max_row_landed")
        den_in = sem("den_landed")
        rec_done = sem("reciprocal_done")
        rscr_in = sem("reciprocal_in_dram")
        rb_in = sem("reciprocal_spread")
        norm_done = sem("z_normalised")
        s3_stats = sem("s3_stats_ready")
        s3_eps = sem("s3_var_eps")
        s3_rstd = sem("s3_rstd_ready")
        s3_h3 = sem("s3_normalised")
        s3_chain = sem("s3_dve_chain")
        s3_top = sem("s3_top_logit")
        s3_score = sem("s3_score_tanh")
        s3_tanh = sem("s3_gate_tanh")
        s3_oh = sem("s3_onehot")
        s3_st = sem("s3_bn_stats")
        routed_in = [sem("record_written_even"), sem("record_written_odd")]
        table = sem("tile_table_chain")
        blank_in = sem("blank_rows_written")
        rec_in = [sem(f"tile_landed_{r}") for r in range(RING)]
        out_in = [sem(f"tile_written_{r}") for r in range(RING)]
        ft_ready = sem("tile_turned")
        ft_copied = sem("tile_turned_copied")
        gu_ready = sem("gate_up_ready")
        gu_tanh = sem("gate_tanh")
        act_half = sem("activation_half")
        act_done = sem("activation_done")
        at_ready = sem("activation_turned")
        at_copied = sem("activation_turned_copied")
        dn_ready = sem("down_ready")
        y_done = sem("y_done")

        S1_USES = 14
        ACT_USES = [0, 5, 10, 13]
        DVE_USES = [1, 2, 3, 4, 6, 7, 8, 9, 11, 12]

        def consumed(G, u):
            if u < 0:
                G, u = G.plus(-1), u + S1_USES
            if u in ACT_USES:
                return s1_act, len(ACT_USES) * G.number + ACT_USES.index(u) + 1
            return s1_dve, len(DVE_USES) * G.number + DVE_USES.index(u) + 1

        def produced(G, u):
            return S1_USES * G.number + u + 1

        PRO_Y = XH // 4
        PRO_USES = PRO_Y + NC + 1
        SLOTS = B + 2

        def does(n, part):
            if not isinstance(n, int):
                return True
            lead = {"scores": 0, "max": 1, "out": -1, "ffn": -2}[part]
            return 0 <= n + lead < B

        def has_y(n, b):
            return b % 2 == 0 and (not isinstance(n, int) or n + 2 < B)

        def slot_uses(n, b):
            uses = [("stm", c) for c in range(NC)] if does(n, "max") else []
            uses += [("f", 0)] if does(n, "ffn") else []
            uses += [("mt", 0)] if does(n, "max") else []
            uses += [("f", 1), ("f", 2)] if does(n, "ffn") else []
            uses += [("y", 0), ("y", 1)] if has_y(n, b) else []
            uses += [("f", 3)] if does(n, "ffn") else []
            uses += [("y", 2), ("y", 3)] if has_y(n, b) else []
            uses += [("f", 4), ("f", 5)] if does(n, "ffn") else []
            uses += [("out", 0)] if does(n, "out") else []
            return uses

        SLOT_OFF = [sum(len(slot_uses(None, k)) for k in range(b)) for b in range(GB)]
        PER_G = sum(len(slot_uses(None, k)) for k in range(GB))
        FIRST_G = PRO_USES + sum(len(slot_uses(n, n)) for n in range(GB))

        def base(g, b):
            if isinstance(g, int):
                return PRO_USES + sum(len(slot_uses(n, n % GB)) for n in range(GB * g + b))
            return PER_G * g + (FIRST_G - PER_G + SLOT_OFF[b])

        def use_index(G, b, kind, i=0):
            g = G.number
            n = g * GB + b
            pos = slot_uses(n if isinstance(n, int) else None, b).index((kind, i))
            even = base(g, b) if isinstance(g, int) else FIRST_G + PER_G + SLOT_OFF[b]
            return base(g, b) + pos, 2 + (even + pos) % 2

        def z_slot_uses(n, b):
            if not has_y(n, b):
                return ["z0", "z1", "z2", "z3"]
            return ["z0", "z1", "y0", "y1", "z2", "y2", "y3", "z3"]

        Z_OFF = [sum(len(z_slot_uses(None, k)) for k in range(b)) for b in range(GB)]
        Z_PER_G = sum(len(z_slot_uses(None, k)) for k in range(GB))

        def z_base(G, b):
            g, b = G.number + b // GB, b % GB
            if isinstance(g, int):
                return PRO_Y + sum(len(z_slot_uses(n, n % GB)) for n in range(min(GB * g + b, B)))
            return Z_PER_G * g + (PRO_Y + Z_OFF[b])

        def z_use(G, b, kind):
            n = G.number * GB + b
            pos = z_slot_uses(n if isinstance(n, int) else None, b % GB).index(kind)
            return z_base(G, b) + pos, 6 + pos % 2

        def over_groups(engine, body):
            body(GroupIndex(0, 0, 0), GB)
            with engine.Fori(0, (NG - 4) // 2) as i:
                body(GroupIndex(i * 2 + 1, 1, i), GB)
                body(GroupIndex(i * 2 + 2, 0, i + 1), GB)
            for g in range(NG - 3, NG):
                body(GroupIndex(g, g % 2, g // 2), GB)
            body(GroupIndex(NG, NG % 2, NG // 2), SLOTS - B)

        PE_STEPS = {(2, "D"): "turn x", (3, "A"): "project first pair", (3, "C"): "project second pair",
                    (3, "D"): "project q",
                    (0, "A"): "k^T v", (0, "C"): "q k^T v", (1, "C"): "turn gated", (1, "D"): "output",
                    (2, "B"): "turn x1 and context"}
        DVE_STEPS = {(2, "A"): "split x1^T", (2, "B"): "stats of x", (2, "C"): "normalise x", (3, "A"): "first pair", (3, "C"): "second pair",
                     (0, "A"): "mask", (0, "D"): "attention", (0, "E"): "gating, first half",
                     (1, "A"): "gating, second half", (1, "E"): "x1",
                     (2, "0"): "normalise x1"}
        ACT_STEPS = {(2, "D"): "copy x^T", (3, "D"): "sigmoids", (1, "C"): "copy gated^T",
                     (2, "B"): "copy x1^T", (2, "C"): "copy context"}
        POOL_STEPS = {(2, "A"): "rstd of x", (0, "0"): "gate terms", (0, "E"): "rstd of attention",
                      (1, "E"): "rstd of x1", (2, "0"): "residual"}
        FINISHING = ("normalise x1", "split x1^T", "turn x1 and context", "copy x1^T", "copy context", "residual")

        def s1_step(run, engine, steps, G, b, place):
            name = steps.get((b, place))
            ahead = 1 if b < 2 or name in FINISHING else 2
            if name is not None and not is_last(G, ahead):
                run(engine, G.plus(ahead), name)

        def is_last(G, k=1):
            return isinstance(G.number, int) and G.number + k > NG - 1

        def routed_before(G, b):
            return 16 * (G.number * 2 + b // 2 - 1)

        TABLE_CHAIN = 14

        def tile_runs(j, lag):
            return not isinstance(j, int) or 0 <= j - lag < TILES

        def over_tiles(engine, step):
            for j in range(RING):
                step(j, j, 0)
            with engine.Fori(1, TILES // RING) as i:
                for k in range(RING):
                    step(i * RING + k, k, i)
            for k in range(3):
                step(TILES + k, k, TILES // RING)

        pre = GroupIndex(0, 0, 0)
        CONSTS_FIRST = 3
        CONSTS_S1 = CONSTS_FIRST + 2 + D // AH + 1
        CONSTS = CONSTS_S1 + 16
        S3_CHAIN = 9
        CHAIN_AT = {"stats of x": 0, "attention": 1, "gating, first half": 4,
                    "gating, second half": 5, "x1": 5}
        CHAIN = 6
        rawq = pT[:, 0, 0:INNER]
        rawk = pT[0:DE, 0, INNER:2 * INNER]
        rawv = pT[0:DE, 1, 0:INNER]
        rawo = pT[:, 1, INNER:2 * INNER].rearrange("p (j n) -> p j n", n=D)
        wqT = rb[:, 0, 0:1024].rearrange("p (j n) -> p j n", n=P)
        wkT = rb[:, 0, 1024:1024 + 8 * DE].rearrange("p (j n) -> p j n", n=DE)
        wvT = rb[:, 1, 0:8 * DE].rearrange("p (j n) -> p j n", n=DE)

        block = ctx.enter_context(nc.Block())

        def load_x(eng, G):
            if isinstance(G.number, int):
                src = x[GB * G.number:GB * G.number + GB]
            else:
                src = x[bass.ds(G.number * GB, GB)]
            eng.dma_start(xin[:, G.parity], src.rearrange("b s d -> s b d")).then_inc(x_in[G.parity], 16)

        def load_ctx(eng, G):
            if isinstance(G.number, int):
                src = ctx_in[GB * G.number:GB * G.number + GB]
            else:
                src = ctx_in[bass.ds(G.number * GB, GB)]
            eng.dma_start(ctx_nat[:, G.parity, :, 0:DE], src.rearrange("b s d -> s b d"))\
                .then_inc(c_in[G.parity], 16)

        @block.sync
        def _(sp):
            load_x(sp, pre)
            sp.dma_start(wkvh[:, 0:D], Wh).then_inc(w_in, 16)
            sp.dma_start(wkvh[:, D:2 * D], Wk).then_inc(w_in, 16)
            sp.dma_start(wkvh[:, 2 * D:], Wv).then_inc(w_in, 16)
            sp.dma_start(wq[:], Wq).then_inc(w_in, 16)
            sp.dma_start(bq_col[:], bq.rearrange("(p o) -> p o", o=1)).then_inc(w_in, 16)
            sp.dma_start(rawq, XWq).then_inc(wx_in, 16)
            sp.dma_start(rawk, XWk).then_inc(wx_in, 16)
            sp.dma_start(rawv, XWv).then_inc(wx_in, 16)
            sp.dma_start(rawo, XWo.rearrange("(j p) n -> p j n", p=P)).then_inc(wo_in, 16)
            sp.dma_start(wo[:], Wo).then_inc(wo_in, 16)
            load_ctx(sp, pre)
            load_x(sp, pre.plus(1))
            load_ctx(sp, pre.plus(1))
            sp.dma_start(gate[:], gate_w).then_inc(wm_in, 16)
            sp.dma_start(sh_gu[:, 0:I], sh_gate).then_inc(wm_in, 16)
            sp.dma_start(sh_gu[:, I:], sh_up).then_inc(wm_in, 16)
            sp.dma_start(sh_dn[:], sh_down.rearrange("(k p) n -> p k n", p=P)).then_inc(wm_in, 16)
            gu_v = rt_gu[:].rearrange("p (e c) -> p e c", e=E)
            sp.dma_start(gu_v[:, :, 0:I], rt_gate.rearrange("e h i -> h e i")).then_inc(wm_in, 16)
            sp.dma_start(gu_v[:, :, I:], rt_up.rearrange("e h i -> h e i")).then_inc(wm_in, 16)
            sp.dma_start(rt_dn[:].rearrange("p (k n) -> p k n", n=D),
                         rt_down.rearrange("e (k p) n -> p (e k) n", p=P)).then_inc(wm_in, 16)
            sp.wait_ge(consts, CONSTS)
            sp.dma_start(routed[E * REGION:E * REGION + P, :], blank[:]).then_inc(blank_in, 16)

            def max_row(n, b, count):
                sp.wait_ge(rot_free, count + 1)
                if by_register(count + 1):
                    sp.sem_inc(waited, 1)
                if due((n - GB + 1) * NC):
                    sp.wait_ge(st_ready, (n - GB + 1) * NC)
                    if by_register((n - GB + 1) * NC):
                        sp.sem_inc(waited, 1)
                sp.dma_start(Y[DE:DE + 1, b % GB], mrow[:, b % 2, :]).then_inc(mrow_in, 16)

            def spread_reciprocal(G, n, b):
                r = b % 2
                sp.wait_ge(z_evac, z_base(G, b + 1))
                if by_register(z_base(G, b + 1)):
                    sp.sem_inc(waited, 1)
                sp.dma_start(den[:, r, :], zs[DE:DE + 1, r, :]).then_inc(den_in, 16)
                sp.wait_ge(rec_done, n + 1)
                if by_register(n + 1):
                    sp.sem_inc(waited, 1)
                row = r_scratch[n:n + 1] if isinstance(n, int) else r_scratch[bass.ds(n, 1)]
                sp.dma_start(row.rearrange("o (p q) -> (o p) q", q=XH), rrec[:, r, :]).then_inc(rscr_in, 16)
                sp.wait_ge(rscr_in, (n + 1) * 16)
                if by_register((n + 1) * 16):
                    sp.sem_inc(waited, 1)
                if due((n - 1) * NC):
                    sp.wait_ge(norm_done, (n - 1) * NC)
                    if by_register((n - 1) * NC):
                        sp.sem_inc(waited, 1)
                if due(n * 16):
                    sp.wait_ge(rb_in, n * 16)
                    if by_register(n * 16):
                        sp.sem_inc(waited, 1)
                sp.dma_start(rb[0:DE, r, :], row.rearrange("o f -> (o f)").partition_broadcast(DE))\
                    .then_inc(rb_in, 16)

            max_row(0, 0, PRO_USES - 1)

            def body(G, slots):
                for b in range(slots):
                    n = G.number * GB + b
                    if does(n, "max"):
                        max_row(n + 1, b + 1, use_index(G, b, "mt")[0])
                    if does(n, "scores"):
                        spread_reciprocal(G, n, b)
                    if b == 3 and not is_last(G, 3):
                        sp.wait_ge(s1_x1b, G.number + 2)
                        if by_register(G.number + 2):
                            sp.sem_inc(waited, 1)
                        load_x(sp, G.plus(3))
                    if b == 3 and not is_last(G, 2):
                        load_ctx(sp, G.plus(2))

            sp.wait_ge(s1_x1b, 1)
            if by_register(1):
                sp.sem_inc(waited, 1)
            load_x(sp, pre.plus(2))
            over_groups(sp, body)

            sp.wait_ge(table, 1)
            if by_register(1):
                sp.sem_inc(waited, 1)
            for e in range(0, E, 2):
                tail = sp.value_load(tail_i[0:1, e:e + 1], min_val=e * REGION, max_val=e * REGION + TOKENS)
                sp.dma_start(routed[bass.ds(tail, P), :], blank[:]).then_inc(blank_in, 16)
            sp.wait_ge(blank_in, 16 * (E + 1))
            if by_register(16 * (E + 1)):
                sp.sem_inc(waited, 1)
            sp.wait_ge(routed_in[0], 16 * B // 2)
            if by_register(16 * B // 2):
                sp.sem_inc(waited, 1)
            sp.wait_ge(routed_in[1], 16 * B // 2)
            if by_register(16 * B // 2):
                sp.sem_inc(waited, 1)
            sp.wait_ge(table, TABLE_CHAIN)
            if by_register(TABLE_CHAIN):
                sp.sem_inc(waited, 1)

            def load_tile(j, r, turn):
                if due(16 * turn):
                    sp.wait_ge(out_in[r], 16 * turn)
                    if by_register(16 * turn):
                        sp.sem_inc(waited, 1)
                at = row_tab[0:1, j:j + 1] if isinstance(j, int) else row_tab[0:1, bass.ds(j, 1)]
                first_row = sp.value_load(at, min_val=0, max_val=E * REGION)
                sp.dma_start(rec[:, r, :], routed[bass.ds(first_row, P), :]).then_inc(rec_in[r], 16)

            for r in range(RING):
                load_tile(r, r, 0)
            with sp.Fori(1, TILES // RING) as i:
                for r in range(RING):
                    load_tile(i * RING + r, r, i)

        def s1_rstd_pool(pool, G, k):
            pool.wait_ge(s1_stats, 3 * G.number + k + 1)
            if by_register(3 * G.number + k + 1):
                pool.sem_inc(waited, 1)
            nc.gpsimd.tensor_scalar(var_eps[:], mv[:, :, 1], EPS, None, ALU.add).then_inc(s1_eps, 1)
            pool.wait_ge(s1_eps, 3 * G.number + k + 1)
            nc.gpsimd.tensor_tensor(rstd[:], var_eps[:], neg_half[:], ALU.pow).then_inc(s1_rstd, 1)

        def s1_pool(pool, G, step):
            if step == "rstd of x":
                s1_rstd_pool(pool, G, 0)
            if step == "gate terms":
                pool.wait_ge(s1_dve, len(DVE_USES) * G.number + 4)
                nc.gpsimd.tensor_tensor(hw[:], hkv[:, :, 0:D], spread(lnw_bc[:], 1, GB), ALU.mult)
                nc.gpsimd.tensor_tensor(hb[:], hkv[:, :, 0:D], spread(lnb_bc[:], 1, GB), ALU.mult)\
                    .then_inc(s1_gate, 1)
            if step == "rstd of attention":
                s1_rstd_pool(pool, G, 1)
            if step == "rstd of x1":
                s1_rstd_pool(pool, G, 2)
            if step == "residual":
                pool.wait_ge(s1_x1, G.number + 1)
                nc.gpsimd.tensor_tensor(x1b[:, G.parity], x1[:], spread(xbo_bc[:], 1, GB), ALU.add)\
                    .then_inc(s1_x1b, 1)

        @block.gpsimd
        def _(pool):
            nc.gpsimd.memset(neg_half[:], -0.5).then_inc(consts, 1)
            nc.gpsimd.memset(ident[:], 0.0).then_inc(consts, 1)
            pool.wait_ge(consts, 2)
            nc.gpsimd.affine_select(out=ident[:], in_=ident[:], compare_op=ALU.not_equal, fill=1.0, base=0,
                                    pattern=[[-1, P]], channel_multiplier=1).then_inc(consts, 1)
            nc.gpsimd.memset(hkv[:, :, 3 * D:], 1.0).then_inc(consts, 1)
            nc.gpsimd.memset(head_mask[:], 0.0).then_inc(consts, 1)
            hm = head_mask[:].rearrange("p (m h) -> p m h", h=AH)
            for d in range(D // AH):
                pool.wait_ge(consts, CONSTS_FIRST + 2 + d)
                nc.gpsimd.affine_select(out=hm, in_=hm, compare_op=ALU.not_equal, fill=1.0, base=-AH * d,
                                        pattern=[[0, KVW // AH], [-1, AH]], channel_multiplier=1)\
                    .then_inc(consts, 1)
            s1_pool(pool, pre, "rstd of x")
            pool.wait_ge(wb_in, 16 * 4)
            nc.gpsimd.tensor_tensor(b_hkv[:, 0:D], b_hkv[:, 0:D], beta_bc[:], ALU.add).then_inc(consts, 1)
            nc.gpsimd.memset(ctx_nat[:, :, :, DE:DE + 1], 1.0).then_inc(consts, 1)
            pool.wait_ge(consts, CONSTS_S1 + 1)
            nc.gpsimd.memset(ctxT[DE:DE + 1], 1.0).then_inc(consts, 1)
            pool.wait_ge(consts, CONSTS_S1 + 2)
            nc.gpsimd.memset(before[:], 1.0).then_inc(consts, 1)
            pool.wait_ge(consts, CONSTS_S1 + 3)
            nc.gpsimd.affine_select(out=before[:], in_=before[:], compare_op=ALU.is_gt, fill=0.0, base=0,
                                    pattern=[[1, P]], channel_multiplier=-1).then_inc(consts, 1)
            nc.gpsimd.memset(ones16[:], 1.0).then_inc(consts, 1)
            ramp = dict(base=0, channel_multiplier=0, allow_small_or_imprecise_dtypes=True)
            nc.gpsimd.iota(expert_no[:], [[1, E]], **ramp).then_inc(consts, 1)
            nc.gpsimd.iota(next_row[:], [[REGION, E]], **ramp).then_inc(consts, 1)
            nc.gpsimd.iota(token_no[:], [[0, 1]], base=0, channel_multiplier=1,
                           allow_small_or_imprecise_dtypes=True).then_inc(consts, 1)
            nc.gpsimd.memset(blank[:, 0:2 * D], 0.0).then_inc(consts, 1)
            nc.gpsimd.iota(blank[:, 2 * D:].bitcast(I32), [[0, 1]], base=TOKENS, channel_multiplier=1)\
                .then_inc(consts, 1)
            pool.wait_ge(wl_in, 16 * 4)
            s1_pool(pool, pre, "gate terms")
            pool.wait_ge(s1_gate, 1)
            pool.wait_ge(consts, CONSTS - 6)
            nc.gpsimd.iota(region[:], [[REGION, E]], **ramp).then_inc(consts, 1)
            pool.wait_ge(consts, CONSTS - 5)
            nc.gpsimd.iota(steps[:], [[0, E], [P, TOKENS // P]], **ramp).then_inc(consts, 1)
            pool.wait_ge(consts, CONSTS - 4)
            nc.gpsimd.iota(tile_no[:], [[1, TILES], [0, E]], **ramp).then_inc(consts, 1)
            pool.wait_ge(consts, CONSTS - 3)
            nc.gpsimd.iota(tile_off[:], [[P, TILES]], **ramp).then_inc(consts, 1)
            pool.wait_ge(consts, CONSTS - 2)
            nc.gpsimd.memset(upto[:], 1.0).then_inc(consts, 1)
            pool.wait_ge(consts, CONSTS - 1)
            nc.gpsimd.affine_select(out=upto[:], in_=upto[:], compare_op=ALU.is_ge, fill=0.0, base=0,
                                    pattern=[[1, E], [-1, E]], channel_multiplier=0).then_inc(consts, 1)
            s1_pool(pool, pre, "rstd of attention")
            s1_pool(pool, pre, "rstd of x1")
            s1_pool(pool, pre, "residual")
            s1_pool(pool, pre.plus(1), "rstd of x")

            def normalise(n, b, c):
                cols = slice(c * CH * S, (c + 1) * CH * S)
                if c == 0:
                    pool.wait_ge(rb_in, (n + 1) * 16)
                nc.gpsimd.tensor_tensor(zs[0:DE, b % 2, cols], zs[0:DE, b % 2, cols], rb[0:DE, b % 2, cols],
                                        ALU.mult).then_inc(norm_done, 1)

            def rstd_of_x2(m):
                pool.wait_ge(s3_stats, m + 1)
                if by_register(m + 1):
                    pool.sem_inc(waited, 1)
                nc.gpsimd.tensor_scalar(var3[:], mv3[:, 1:2], EPS, None, ALU.add).then_inc(s3_eps, 1)
                pool.wait_ge(s3_eps, m + 1)
                nc.gpsimd.tensor_tensor(rstd3[:], var3[:], neg_half[:, 0:1], ALU.pow).then_inc(s3_rstd, 1)

            def scatter_records(count, r):
                pool.wait_ge(rot_free, count + 1)
                if by_register(count + 1):
                    pool.sem_inc(waited, 1)
                pool.indirect_dma_start(routed, bass.IndirectOffsetOnAxis(ap=row_i[:, r:r + 1], axis=0),
                                        record[:, r, :], None).then_inc(routed_in[r], 16)

            def body(G, slots):
                for b in range(slots):
                    n = G.number * GB + b
                    s1_step(s1_pool, pool, POOL_STEPS, G, b, "0")
                    s1_step(s1_pool, pool, POOL_STEPS, G, b, "A")
                    if does(n, "out"):
                        for c in range(NC):
                            normalise(n - 1, b + 1, c)
                    s1_step(s1_pool, pool, POOL_STEPS, G, b, "E")
                    if does(n, "ffn"):
                        scatter_records(use_index(G, b, "f", 5)[0], b % 2)
                    if does(n, "out"):
                        rstd_of_x2(n - 1)

            over_groups(pool, body)

            def store_tile(j, r):
                pool.wait_ge(y_done, j + 1)
                if by_register(j + 1):
                    pool.sem_inc(waited, 1)
                pool.indirect_dma_start(
                    out.rearrange("b s d -> (b s) d"),
                    bass.IndirectOffsetOnAxis(ap=rec[:, r, 2 * D:].bitcast(I32), axis=0),
                    yo[:, r, :], None, bounds_check=TOKENS - 1, oob_is_err=False).then_inc(out_in[r], 16)

            for r in range(RING):
                store_tile(r, r)
            with pool.Fori(1, TILES // RING) as i:
                for r in range(RING):
                    store_tile(i * RING + r, r)
            for r in range(RING):
                pool.wait_ge(out_in[r], 16 * (TILES // RING))

        def s1_dve_fn(dve, G, step):
            count = [CHAIN_AT.get(step, 0)]

            def link(ins):
                ins.then_inc(s1_chain, 1)
                count[0] += 1
                dve.wait_ge(s1_chain, CHAIN * G.number + count[0])
                if by_register(CHAIN * G.number + count[0]):
                    dve.sem_inc(waited, 1)

            def emptied(u):
                dve.wait_ge(s1_pe, produced(G, u))
                return bank[u % 2]

            def stats_of(src):
                for b in range(GB):
                    last = nc.vector.bn_stats(stats[:, b, :], src[:, b, :])
                link(last)
                for b in range(GB):
                    last = nc.vector.bn_aggr(mv[:, b, :], stats[:, b, :])
                last.then_inc(s1_stats, 1)

            def normalise(dst, src, k):
                dve.wait_ge(s1_rstd, 3 * G.number + k + 1)
                for b in range(GB):
                    last = nc.vector.tensor_scalar(dst[:, b, :], src[:, b, :], mv[:, b, 0:1], rstd[:, b:b + 1],
                                                   ALU.subtract, ALU.mult)
                last.then_inc(s1_xn, 1)

            if step == "stats of x":
                dve.wait_ge(x_in[G.parity], 16 * (G.half + 1))
                stats_of(xin[:, G.parity])
            if step == "normalise x":
                normalise(xn, xin[:, G.parity], 0)
            if step == "split x1^T":
                ps = emptied(12)
                dve.wait_ge(s1_hi, G.number + 1)
                nc.vector.tensor_tensor(xn2T_lo[:, G.parity], ps[:], xn2T_hi[:, G.parity].bitcast(F32), ALU.subtract)\
                    .then_inc(s1_dve, 1)
            if step in ("first pair", "second pair"):
                for u in ((1, 2) if step == "first pair" else (3, 4)):
                    ps = emptied(u)
                    if u == 1:
                        if due(G.number):
                            dve.wait_ge(s1_gate, G.number)
                    nc.vector.tensor_tensor(hkv[:, u - 1, 0:3 * D], ps[:, 0:3 * D], b_hkv[:], ALU.add)\
                        .then_inc(s1_dve, 1)
            if step == "mask":
                for u in (6, 7):
                    ps = emptied(u)
                    for j in range(2):
                        last = nc.vector.tensor_tensor(kvm[:, 2 * (u - 6) + j, :], ps[:, j * KVW:(j + 1) * KVW],
                                                       head_mask[:], ALU.mult)
                    last.then_inc(s1_dve, 1)
            if step == "attention":
                for u in (8, 9):
                    ps = emptied(u)
                    v = ps[:, 0:2 * KVW].rearrange("p (b n) -> p b n", n=KVW)
                    b0 = 2 * (u - 8)
                    link(nc.vector.reciprocal(rden[:, b0:b0 + 2, :], v[:, :, D:KVW]))
                    for j in range(2):
                        last = nc.vector.tensor_tensor(
                            attn[:, b0 + j, :].rearrange("p (m h) -> p m h", h=AH),
                            v[:, j, 0:D].rearrange("p (m h) -> p m h", h=AH),
                            spread(rden[:, b0 + j, :], 1, D // AH), ALU.mult)
                    last.then_inc(s1_dve, 1)
                dve.wait_ge(s1_dve, len(DVE_USES) * G.number + 8)
                stats_of(attn)
            if step == "gating, first half":
                dve.wait_ge(s1_stats, 3 * G.number + 2)
                dve.wait_ge(s1_gate, G.number + 1)
                for b in range(GB):
                    last = nc.vector.scalar_tensor_tensor(out=attn[:, b, :], in0=attn[:, b, :],
                                                          scalar=mv[:, b, 0:1], in1=hw[:, b, :],
                                                          op0=ALU.subtract, op1=ALU.mult)
                link(last)
            if step == "gating, second half":
                dve.wait_ge(s1_rstd, 3 * G.number + 2)
                for b in range(GB):
                    last = nc.vector.scalar_tensor_tensor(out=attn[:, b, :], in0=attn[:, b, :],
                                                          scalar=rstd[:, b:b + 1], in1=hb[:, b, :],
                                                          op0=ALU.mult, op1=ALU.add)
                last.then_inc(s1_xn, 1)
            if step == "x1":
                ps = emptied(11)
                if due(G.number):
                    dve.wait_ge(s1_x1b, G.number)
                t = ps[:].rearrange("p (b n) -> p b n", n=D)
                nc.vector.tensor_tensor(x1[:], t, spread(bo_bc[:], 1, GB), ALU.add).then_inc(s1_dve, 1)
                dve.wait_ge(s1_dve, len(DVE_USES) * G.number + DVE_USES.index(11) + 1)
                nc.vector.scalar_tensor_tensor(out=x1[:], in0=x1[:], scalar=0.0, in1=xin[:, G.parity],
                                               op0=ALU.max, op1=ALU.add).then_inc(s1_x1, 1)
                dve.wait_ge(s1_x1, G.number + 1)
                stats_of(x1)
            if step == "normalise x1":
                normalise(xn, x1, 2)

        @block.vector
        def _(dve):
            s1_dve_fn(dve, pre, "stats of x")
            s1_dve_fn(dve, pre, "normalise x")
            dve.wait_ge(consts, CONSTS_S1)
            s1_dve_fn(dve, pre, "first pair")
            s1_dve_fn(dve, pre, "second pair")
            for k in range(2):
                dve.wait_ge(su_pe, k + 1)
                nc.vector.tensor_copy(wqT[:, 4 * k:4 * k + 4, :],
                                      bank[2 + k][:].rearrange("p (j n) -> p j n", n=P)).then_inc(su_dve, 1)
            for k in range(2):
                dve.wait_ge(su_pe, 3 + k)
                nc.vector.tensor_copy(wkT[:, 4 * k:4 * k + 4, :],
                                      bank[4 + k][:, 0:4 * DE].rearrange("p (j n) -> p j n", n=DE))\
                    .then_inc(su_dve, 1)
            s1_dve_fn(dve, pre, "mask")
            s1_dve_fn(dve, pre, "attention")
            s1_dve_fn(dve, pre, "gating, first half")
            s1_dve_fn(dve, pre, "gating, second half")
            dve.wait_ge(wl_in, 16 * 4)
            s1_dve_fn(dve, pre, "x1")
            s1_dve_fn(dve, pre, "normalise x1")
            for half in range(2):
                for odd in range(2):
                    dve.wait_ge(su_act, 3 + 2 * half + odd)
                    ps = bank[2 + 2 * half + odd][:, 0:4 * DE].rearrange("p (j n) -> p j n", n=DE)
                    heads = slice(8 * half + odd, 8 * half + 8, 2)
                    nc.vector.tensor_tensor(A_lo[:, heads, :], ps, A_hi[:, heads, :].bitcast(F32), ALU.subtract)\
                        .then_inc(su_dve, 1)
            s1_dve_fn(dve, pre, "split x1^T")
            dve.wait_ge(consts, CONSTS)

            def y_out(count, bk, r0, i):
                dve.wait_ge(rot_ready, count + 1)
                src = bank[bk][0:DE, :].rearrange("p (h b t) -> p h b t", h=2, b=2)
                dst = Y[0:DE, r0:r0 + 2, 2 * i:2 * i + 2, :].rearrange("p b h t -> p h b t")
                nc.vector.tensor_copy(dst, src).then_inc(rot_free, 1)

            def head_max(count, bk, b, c):
                dve.wait_ge(rot_ready, count + 1)
                nc.vector.tensor_reduce(mneg[:, b % 2, c * CH:(c + 1) * CH],
                                        bank[bk][:].rearrange("p (h k) -> p h k", h=CH),
                                        AX.X, ALU.max, negate=True).then_inc(rot_free, 1)

            def max_copy(count, bk, n, b):
                dve.wait_ge(rot_ready, count + 1)
                if due((n - 1) * 16):
                    dve.wait_ge(mrow_in, (n - 1) * 16)
                nc.vector.tensor_copy(mrow[:, b % 2, :], bank[bk][0:XH, 0:S]).then_inc(rot_free, 1)

            for i in range(PRO_Y):
                y_out(i, 2 + i % 2, 0, 2 * i)
                if i == 1:
                    s1_dve_fn(dve, pre.plus(1), "stats of x")
            s1_dve_fn(dve, pre.plus(1), "normalise x")
            for c in range(NC):
                head_max(PRO_Y + c, 2 + c % 2, 0, c)
            s1_dve_fn(dve, pre.plus(1), "first pair")
            max_copy(PRO_USES - 1, 2 + (PRO_USES - 1) % 2, 0, 0)
            s1_dve_fn(dve, pre.plus(1), "second pair")

            def reciprocal(n, b):
                dve.wait_ge(den_in, (n + 1) * 16)
                if due((n - 1) * 16):
                    dve.wait_ge(rscr_in, (n - 1) * 16)
                nc.vector.reciprocal(rrec[:, b % 2, :], den[:, b % 2, :]).then_inc(rec_done, 1)

            def residual(count, bk, n, parity, b):
                dve.wait_ge(rot_ready, count + 1)
                nc.vector.tensor_tensor(x2[:, b % 2, :], bank[bk][:, 0:D], x1b[:, parity, b, :], ALU.add)\
                    .then_inc(rot_free, 1)
                dve.wait_ge(rot_free, count + 1)
                nc.vector.bn_stats(st3[:], x2[:, b % 2, :]).then_inc(s3_st, 1)
                dve.wait_ge(s3_st, n + 1)
                if by_register(n + 1):
                    dve.sem_inc(waited, 1)
                nc.vector.bn_aggr(mv3[:], st3[:]).then_inc(s3_stats, 1)

            def ffn(G, b, m, step):
                r = b % 2
                done = [{"logits": 0, "gate_up": 3, "rank": 4, "scale": 7}.get(step, 0)]

                def link(ins):
                    ins.then_inc(s3_chain, 1)
                    done[0] += 1
                    dve.wait_ge(s3_chain, S3_CHAIN * m + done[0])
                    if by_register(S3_CHAIN * m + done[0]):
                        dve.sem_inc(waited, 1)

                def use(i):
                    count, bk = use_index(G, b, "f", i)
                    dve.wait_ge(rot_ready, count + 1)
                    return count, bank[bk]

                if step == "normalise":
                    dve.wait_ge(s3_rstd, m + 1)
                    nc.vector.tensor_scalar(h3[:, r, :], x2[:, r, :], mv3[:, 0:1], rstd3[:], ALU.subtract,
                                            ALU.mult).then_inc(s3_h3, 1)
                if step == "turned":
                    count, ps = use(0)
                    nc.vector.tensor_copy(h3T[:], ps[:, 0:S]).then_inc(rot_free, 1)
                if step == "logits":
                    count, ps = use(1)
                    nc.vector.tensor_copy(logits[:], ps[:, 0:E]).then_inc(rot_free, 1)
                    dve.wait_ge(rot_free, count + 1)
                    if by_register(count + 1):
                        dve.sem_inc(waited, 1)
                    link(nc.vector.max(top8[:], logits[:]))
                    link(nc.vector.max_index(idx8[:], top8[:], logits[:]))
                    link(nc.vector.tensor_copy(pick[:], idx8[:, 0:1]))
                    nc.vector.tensor_scalar(onehot[:], expert_no[:], pick[:], None, ALU.is_equal)\
                        .then_inc(s3_oh, 1)
                if step == "gate_up":
                    count, ps = use(2)
                    dve.wait_ge(s3_tanh, m + 1)
                    link(nc.vector.scalar_tensor_tensor(out=act3[:], in0=tanh3[:], scalar=1.0, in1=ps[:, 0:I],
                                                        op0=ALU.add, op1=ALU.mult))
                    nc.vector.scalar_tensor_tensor(out=act3[:], in0=act3[:], scalar=0.5, in1=ps[:, I:2 * I],
                                                   op0=ALU.mult, op1=ALU.mult).then_inc(rot_free, 1)
                if step == "rank":
                    count, ps = use(3)
                    link(nc.vector.tensor_tensor(rank[:], ps[:, 0:E], next_row[:], ALU.add))
                    nc.vector.tensor_tensor(next_row[:], ps[:, E:2 * E], next_row[:], ALU.add)\
                        .then_inc(rot_free, 1)
                    link(nc.vector.tensor_tensor(rank[:], rank[:], onehot[:], ALU.mult))
                    link(nc.vector.tensor_reduce(row_f[:], rank[:], AX.X, ALU.add))
                    if due(routed_before(G, b)):
                        dve.wait_ge(routed_in[r], routed_before(G, b))
                    nc.vector.tensor_copy(row_i[:, r:r + 1], row_f[:])
                if step == "scale":
                    dve.wait_ge(s3_score, m + 1)
                    link(nc.vector.tensor_scalar(score[:, 1:2], score[:, 0:1], 0.5, 0.5, ALU.mult, ALU.add))
                    nc.vector.tensor_scalar(record[:, r, 0:D], h3[:, r, :], score[:, 1:2], None, ALU.mult)
                    link(nc.vector.tensor_copy(record[:, r, 2 * D:].bitcast(I32), token_no[:]))
                    nc.vector.tensor_scalar(token_no[:], token_no[:], float(S), None, ALU.add)
                if step == "act_turned":
                    count, ps = use(4)
                    nc.vector.tensor_copy(act3T[:], ps[:, 0:I]).then_inc(rot_free, 1)
                if step == "shared":
                    count, ps = use(5)
                    nc.vector.tensor_tensor(record[:, r, D:2 * D], ps[:, 0:D], x2[:, r, :], ALU.add)\
                        .then_inc(rot_free, 1)

            def tile_table():
                chain = [1]

                def link(ins):
                    ins.then_inc(table, 1)
                    chain[0] += 1
                    dve.wait_ge(table, chain[0])

                link(nc.vector.tensor_tensor(cnt[:], next_row[0:1, :], region[:], ALU.subtract))
                link(nc.vector.tensor_tensor(over[:], spread(cnt[:], 2, TOKENS // P), steps[:], ALU.is_gt))
                link(nc.vector.tensor_reduce(ntiles[:], over[:], AX.X, ALU.add))
                link(nc.vector.tensor_tensor(part[:], spread(ntiles[:], 1, E), upto[:], ALU.mult))
                link(nc.vector.tensor_reduce(tiles_to[:], part[:], AX.X, ALU.add))
                link(nc.vector.tensor_tensor(passed[:], spread(tiles_to[:], 1, TILES), tile_no[:], ALU.is_le))
                link(nc.vector.tensor_reduce(t_expert[:], passed[:], AX.X, ALU.add))
                link(nc.vector.tensor_tensor(before_t[:], passed[:], spread(ntiles[:], 1, TILES), ALU.mult))
                link(nc.vector.tensor_reduce(t_first[:], before_t[:], AX.X, ALU.add))
                link(nc.vector.scalar_tensor_tensor(out=t_row[:], in0=t_first[:], scalar=-float(P), in1=tile_off[:],
                                                    op0=ALU.mult, op1=ALU.add))
                link(nc.vector.scalar_tensor_tensor(out=t_row[:], in0=t_expert[:], scalar=float(REGION),
                                                    in1=t_row[:], op0=ALU.mult, op1=ALU.add))
                link(nc.vector.tensor_scalar(row_tab[:], t_row[:], float(E * REGION), None, ALU.min))
                link(nc.vector.tensor_scalar(exp_tab[:], t_expert[:], float(E - 1), None, ALU.min))
                assert chain[0] == TABLE_CHAIN

            def body(G, slots):
                for b in range(slots):
                    n = G.number * GB + b
                    m = n - 2
                    f = (lambda step: ffn(G, b, m, step)) if does(n, "ffn") else (lambda step: None)
                    s1 = lambda place: s1_step(s1_dve_fn, dve, DVE_STEPS, G, b, place)

                    def y(i):
                        if has_y(n, b):
                            for k in range(i, i + 2):
                                y_out(*use_index(G, b, "y", k), (b + 2) % GB, 2 * k)

                    if does(n, "out"):
                        reciprocal(n - 1, b + 1)
                    if does(n, "max"):
                        for c in range(NC):
                            head_max(*use_index(G, b, "stm", c), b + 1, c)
                    f("normalise")
                    s1("0")
                    f("turned")
                    if does(n, "max"):
                        max_copy(*use_index(G, b, "mt"), n + 1, b + 1)
                    f("logits")
                    s1("A")
                    s1("B")
                    f("gate_up")
                    y(0)
                    f("rank")
                    if isinstance(n, int) and m == B - 1:
                        nc.vector.tensor_copy(tail_i[:], next_row[0:1, :]).then_inc(table, 1)
                    s1("C")
                    y(2)
                    f("act_turned")
                    f("scale")
                    f("shared")
                    if isinstance(n, int) and m == B - 1:
                        tile_table()
                    s1("D")
                    s1("E")
                    if does(n, "out"):
                        residual(*use_index(G, b, "out"), n - 1, G.parity if b else 1 - G.parity, (b - 1) % GB)

            over_groups(dve, body)

            def activate(j, r2):
                dve.wait_ge(gu_tanh, j + 1)
                ps = bank[2 + r2]
                if due(j - 1):
                    dve.wait_ge(at_ready, j - 1)
                nc.vector.scalar_tensor_tensor(out=act4[:, r2], in0=tanh4[:, r2], scalar=1.0, in1=ps[:, 0:I],
                                               op0=ALU.add, op1=ALU.mult).then_inc(act_half, 1)
                dve.wait_ge(act_half, j + 1)
                nc.vector.scalar_tensor_tensor(out=act4[:, r2], in0=act4[:, r2], scalar=0.5,
                                               in1=ps[:, I:2 * I], op0=ALU.mult, op1=ALU.mult)\
                    .then_inc(act_done, 1)

            def finish(j, r, r2, turn):
                dve.wait_ge(dn_ready, j + 1)
                if due(16 * turn):
                    dve.wait_ge(out_in[r], 16 * turn)
                nc.vector.tensor_tensor(yo[:, r, :], bank[6 + r2][:, 0:D], rec[:, r, D:2 * D], ALU.add)\
                    .then_inc(y_done, 1)

            def step(j, k, turn):
                if tile_runs(j, 1):
                    activate(j - 1, (k - 1) % 2)
                if tile_runs(j, 3):
                    finish(j - 3, (k - 3) % RING, (k - 3) % 2, turn - (1 if k < 3 else 0))

            over_tiles(dve, step)

        def s1_act_fn(act, G, step):
            if step == "copy x^T":
                act.wait_ge(s1_pe, produced(G, 0))
                nc.scalar.copy(xnT[:], bank[0][:]).then_inc(s1_act, 1)
            if step == "sigmoids":
                act.wait_ge(s1_pe, produced(G, 5))
                nc.scalar.activation(qT[:], bank[1][:], ACT.Sigmoid, bias=bq_col[:]).then_inc(s1_act, 1)
                act.wait_ge(s1_dve, len(DVE_USES) * G.number + 4)
                nc.scalar.activation(hkv[:, :, D:2 * D], hkv[:, :, D:2 * D], ACT.Sigmoid).then_inc(s1_ksig, 1)
            if step == "copy gated^T":
                act.wait_ge(s1_pe, produced(G, 10))
                nc.scalar.copy(gT[:], bank[0][:]).then_inc(s1_act, 1)
            if step == "copy x1^T":
                act.wait_ge(s1_pe, produced(G, 12))
                nc.scalar.copy(xn2T_hi[:, G.parity], bank[0][:]).then_inc(s1_hi, 1)
            if step == "copy context":
                act.wait_ge(s1_pe, produced(G, 13))
                nc.scalar.copy(ctxTb[:, G.parity], bank[1][0:DE, :])
                nc.scalar.copy(ctxT[0:DE, G.parity], bank[1][0:DE, :]).then_inc(s1_act, 1)

        @block.scalar
        def _(act):
            bc = lambda v: v.partition_broadcast(P)
            act.dma_start(b_hkv[:, 0:D], bc(bh)).then_inc(wb_in, 16)
            act.dma_start(b_hkv[:, D:2 * D], bc(bk)).then_inc(wb_in, 16)
            act.dma_start(b_hkv[:, 2 * D:], bc(bv)).then_inc(wb_in, 16)
            act.dma_start(beta_bc[:], bc(beta)).then_inc(wb_in, 16)
            act.dma_start(lnw_bc[:], bc(ln_w)).then_inc(wl_in, 16)
            act.dma_start(lnb_bc[:], bc(ln_b)).then_inc(wl_in, 16)
            act.dma_start(bo_bc[:], bc(bo)).then_inc(wl_in, 16)
            act.dma_start(xbo_bc[:], bc(Xbo)).then_inc(wl_in, 16)
            s1_act_fn(act, pre, "copy x^T")
            act.wait_ge(w_in, 16 * 5)
            s1_act_fn(act, pre, "sigmoids")
            for k in range(2):
                act.wait_ge(su_pe, 5 + k)
                nc.scalar.copy(wvT[:, 4 * k:4 * k + 4, :],
                               bank[6 + k][:, 0:4 * DE].rearrange("p (j n) -> p j n", n=DE)).then_inc(su_act, 1)
            for half in range(2):
                for odd in range(2):
                    act.wait_ge(su_pe, 7 + 2 * half + odd)
                    nc.scalar.copy(A_hi[:, 8 * half + odd:8 * half + 8:2, :],
                                   bank[2 + 2 * half + odd][:, 0:4 * DE].rearrange("p (j n) -> p j n", n=DE))\
                        .then_inc(su_act, 1)

            def copy_b(half):
                for odd in range(2):
                    act.wait_ge(su_pe, 11 + 2 * half + odd)
                    nc.scalar.copy(Bw[:, 8 * half + odd:8 * half + 8:2, :],
                                   bank[6 + odd][0:DE, :].rearrange("p (j n) -> p j n", n=D))\
                        .then_inc(su_act, 1)

            copy_b(0)
            s1_act_fn(act, pre, "copy gated^T")
            copy_b(1)
            s1_act_fn(act, pre, "copy x1^T")
            s1_act_fn(act, pre, "copy context")
            for i in range(PRO_Y):
                act.wait_ge(z_ready, i + 1)
                nc.scalar.copy(Y[0:DE, 0:2, 4 * i + 2:4 * i + 4, :].rearrange("p b h t -> p h b t"),
                               bank[6 + i % 2][0:DE, :].rearrange("p (h b t) -> p h b t", h=2, b=2))\
                    .then_inc(z_evac, 1)
            s1_act_fn(act, pre.plus(1), "copy x^T")
            s1_act_fn(act, pre.plus(1), "sigmoids")

            def exp_chunk(G, n, b, c):
                q = n * NC + c
                act.wait_ge(st_ready, q + 1)
                if due(z_use(G, b - 2, f"z{c}")[0] + 1 if not isinstance(n, int) or n >= 2 else 0):
                    act.wait_ge(z_ready, z_use(G, b - 2, f"z{c}")[0] + 1 if not isinstance(n, int) or n >= 2 else 0)
                nc.scalar.activation(pT[:, b % 2, c * CH * S:(c + 1) * CH * S], bank[4 + c % 2][:], ACT.Exp,
                                     scale=float(DH) ** -0.5).then_inc(exp_done, 1)

            def z_copy(G, n, b, c):
                count, bk = z_use(G, b, f"z{c}")
                act.wait_ge(z_ready, count + 1)
                if c == 0:
                    act.wait_ge(rot_ready, base(G.number, b))
                nc.scalar.copy(zs[:, b % 2, c * CH * S:(c + 1) * CH * S], bank[bk][0:DE + 1, :])\
                    .then_inc(z_evac, 1)

            def y_copy(G, b, i):
                count, bk = z_use(G, b, f"y{i}")
                act.wait_ge(z_ready, count + 1)
                r0, h = (b + 2) % GB, 2 * (2 * i + 1)
                nc.scalar.copy(Y[0:DE, r0:r0 + 2, h:h + 2, :].rearrange("p b h t -> p h b t"),
                               bank[bk][0:DE, :].rearrange("p (h b t) -> p h b t", h=2, b=2)).then_inc(z_evac, 1)

            def score_tanh(m):
                act.wait_ge(s3_chain, S3_CHAIN * m + 1)
                nc.scalar.activation(score[:, 0:1], top8[:, 0:1], ACT.Tanh, scale=0.5).then_inc(s3_score, 1)

            def gate_tanh(count, bk):
                act.wait_ge(rot_ready, count + 1)
                nc.scalar.activation(tanh3[:], bank[bk][:, 0:I], ACT.Tanh, scale=0.5).then_inc(s3_tanh, 1)

            def body(G, slots):
                for b in range(slots):
                    n = G.number * GB + b
                    z = (lambda c: z_copy(G, n, b, c)) if does(n, "scores") else (lambda c: None)
                    e = (lambda c: exp_chunk(G, n, b, c)) if does(n, "scores") else (lambda c: None)
                    s1 = lambda place: s1_step(s1_act_fn, act, ACT_STEPS, G, b, place)
                    y = (lambda i: y_copy(G, b, i)) if has_y(n, b) else (lambda i: None)
                    e(0)
                    e(1)
                    z(0)
                    e(2)
                    z(1)
                    s1("B")
                    if does(n, "ffn"):
                        gate_tanh(*use_index(G, b, "f", 2))
                    e(3)
                    y(0)
                    y(1)
                    if does(n, "ffn"):
                        score_tanh(n - 2)
                    z(2)
                    s1("C")
                    y(2)
                    y(3)
                    z(3)
                    s1("D")

            over_groups(act, body)

            act.wait_ge(table, 1)
            for e in range(1, E, 2):
                tail = act.value_load(tail_i[0:1, e:e + 1], min_val=e * REGION, max_val=e * REGION + TOKENS)
                act.dma_start(routed[bass.ds(tail, P), :], blank[:]).then_inc(blank_in, 16)

            def step(j, k, turn):
                if tile_runs(j, 0):
                    act.wait_ge(ft_ready, j + 1)
                    nc.scalar.copy(recT[:, k % 2], bank[k % 2][:, 0:P]).then_inc(ft_copied, 1)
                if tile_runs(j, 1):
                    act.wait_ge(gu_ready, j)
                    if due(j - 2):
                        act.wait_ge(act_done, j - 2)
                    nc.scalar.activation(tanh4[:, (k - 1) % 2], bank[2 + (k - 1) % 2][:, 0:I], ACT.Tanh,
                                         scale=0.5).then_inc(gu_tanh, 1)
                if tile_runs(j, 2):
                    act.wait_ge(at_ready, j - 1)
                    if due(j - 3):
                        act.wait_ge(dn_ready, j - 3)
                    nc.scalar.copy(act4T[:, k % 2], bank[4 + k % 2][:, 0:I]).then_inc(at_copied, 1)

            over_tiles(act, step)

        def s1_pe_fn(pe, G, step):
            def free(u):
                if due(consumed(G, u - 2)[1]):
                    pe.wait_ge(*consumed(G, u - 2))
                return bank[u % 2]

            def turned(u, src, rows, wide=D):
                ps = free(u)
                for b in range(GB):
                    last = pe.transpose(ps[0:wide, b * S:(b + 1) * S], src[:, b, 0:wide], ident[:])
                last.then_inc(s1_pe, 1)

            def project(u):
                ps = free(u)
                b = u - 1
                pe.matmul(ps[:, 0:3 * D], xnT[:, b * S:(b + 1) * S], wkvh[:], start=True, stop=True)\
                    .then_inc(s1_pe, 1)

            if step == "turn x":
                pe.wait_ge(s1_xn, 3 * G.number + 1)
                turned(0, xn, D)
            if step == "project first pair":
                pe.wait_ge(*consumed(G, 0))
                project(1)
                project(2)
            if step == "project second pair":
                project(3)
                project(4)
            if step == "project q":
                pe.matmul(free(5)[:], wq[:], xnT[:], start=True, stop=True).then_inc(s1_pe, 1)
            if step == "k^T v":
                pe.wait_ge(s1_ksig, G.number + 1)
                for u in (6, 7):
                    ps = free(u)
                    for j in range(2):
                        b = 2 * (u - 6) + j
                        last = pe.matmul(ps[:, j * KVW:(j + 1) * KVW], hkv[:, b, D:2 * D], hkv[:, b, 2 * D:],
                                         start=True, stop=True)
                    last.then_inc(s1_pe, 1)
            if step == "q k^T v":
                for u in (8, 9):
                    ps = free(u)
                    pe.wait_ge(*consumed(G, u - 2))
                    for j in range(2):
                        b = 2 * (u - 8) + j
                        last = pe.matmul(ps[:, j * KVW:(j + 1) * KVW], qT[:, b * S:(b + 1) * S], kvm[:, b, :],
                                         start=True, stop=True)
                    last.then_inc(s1_pe, 1)
            if step == "turn gated":
                pe.wait_ge(s1_xn, 3 * G.number + 2)
                turned(10, attn, D)
            if step == "output":
                ps = free(11)
                pe.wait_ge(*consumed(G, 10))
                for b in range(GB):
                    last = pe.matmul(ps[:, b * D:(b + 1) * D], gT[:, b * S:(b + 1) * S], wo[:],
                                     start=True, stop=True)
                last.then_inc(s1_pe, 1)
            if step == "turn x1 and context":
                pe.wait_ge(s1_xn, 3 * G.number + 3)
                turned(12, xn, D)
                pe.wait_ge(c_in[G.parity], 16 * (G.half + 1))
                turned(13, ctx_nat[:, G.parity], DE, DE)

        @block.tensor
        def _(pe):
            pe.wait_ge(consts, CONSTS_FIRST)
            s1_pe_fn(pe, pre, "turn x")
            pe.wait_ge(w_in, 16 * 5)
            s1_pe_fn(pe, pre, "project first pair")
            s1_pe_fn(pe, pre, "project second pair")
            s1_pe_fn(pe, pre, "project q")
            pe.wait_ge(wx_in, 16 * 3)
            for k in range(2):
                for j in range(4):
                    last = pe.transpose(bank[2 + k][:, j * P:(j + 1) * P],
                                        rawq[:, (4 * k + j) * P:(4 * k + j + 1) * P], ident[:])
                last.then_inc(su_pe, 1)
            for w, src in enumerate((rawk, rawv)):
                for k in range(2):
                    for j in range(4):
                        last = pe.transpose(bank[4 + 2 * w + k][:, j * DE:(j + 1) * DE],
                                            src[:, (4 * k + j) * P:(4 * k + j + 1) * P], ident[0:DE, 0:DE])
                    last.then_inc(su_pe, 1)
            s1_pe_fn(pe, pre, "k^T v")
            pe.wait_ge(su_dve, 4)
            for half in range(2):
                if half == 1:
                    s1_pe_fn(pe, pre, "q k^T v")
                for odd in range(2):
                    rows = slice(DH * odd, DH * odd + DH)
                    for j in range(4):
                        last = pe.matmul(bank[2 + 2 * half + odd][:, j * DE:(j + 1) * DE],
                                         wqT[rows, 4 * half + j, :], wkT[rows, 4 * half + j, :],
                                         start=True, stop=True)
                    last.then_inc(su_pe, 1)

            def b_products(half):
                for odd in range(2):
                    rows = slice(DH * odd, DH * odd + DH)
                    for j in range(4):
                        last = pe.matmul(bank[6 + odd][0:DE, j * D:(j + 1) * D],
                                         wvT[rows, 4 * half + j, :], rawo[rows, 4 * half + j, :],
                                         start=True, stop=True)
                    last.then_inc(su_pe, 1)

            pe.wait_ge(su_act, 2)
            pe.wait_ge(wo_in, 16 * 2)
            b_products(0)
            s1_pe_fn(pe, pre, "turn gated")
            pe.wait_ge(su_act, 8)
            b_products(1)
            s1_pe_fn(pe, pre, "output")
            s1_pe_fn(pe, pre, "turn x1 and context")
            pe.wait_ge(su_act, 10)
            pe.wait_ge(su_dve, 8)

            def y_product(count, bk, G, half, i, free=rot_free, ready=rot_ready):
                if due(count - 1):
                    pe.wait_ge(free, count - 1)
                for j in range(2):
                    ps, h = bank[bk][0:DE, j * 256:(j + 1) * 256], 2 * i + j
                    tokens = slice(half * 256, (half + 1) * 256)
                    pe.matmul(ps, A_hi[:, h, :], xn2T_hi[:, G.parity, tokens], start=True, stop=False)
                    pe.matmul(ps, A_hi[:, h, :], xn2T_lo[:, G.parity, tokens], start=False, stop=False)
                    last = pe.matmul(ps, A_lo[:, h, :], xn2T_hi[:, G.parity, tokens], start=False, stop=True)
                last.then_inc(ready, 1)

            def score_rows(count, bk, parity, b, c):
                pe.wait_ge(rot_free, count - 1)
                for j in range(CH):
                    h = c * CH + j
                    y16 = Y[0:DE, b % GB, h, :].bitcast(BF16)[:, 1::2]
                    last = pe.matmul(bank[bk][:, j * S:(j + 1) * S], y16,
                                     ctxTb[:, parity, (b % GB) * S:(b % GB + 1) * S], start=True, stop=True)
                last.then_inc(rot_ready, 1)

            def max_turn(count, bk, last_chunk, b):
                pe.wait_ge(rot_free, last_chunk + 1)
                pe.wait_ge(rot_free, count - 1)
                pe.transpose(bank[bk][0:XH, 0:S], mneg[:, b % 2, :], ident[:]).then_inc(rot_ready, 1)

            pe.wait_ge(*consumed(pre, 12))
            pe.wait_ge(*consumed(pre, 13))
            for i in range(PRO_Y):
                y_product(i, 2 + i % 2, pre, 0, 2 * i)
                y_product(i, 6 + i % 2, pre, 0, 2 * i + 1, z_evac, z_ready)
            pe.wait_ge(rot_free, PRO_Y)
            pe.wait_ge(z_evac, PRO_Y)
            pe.wait_ge(consts, CONSTS)
            for c in range(NC):
                score_rows(PRO_Y + c, 2 + c % 2, 0, 0, c)
                if c == 1:
                    s1_pe_fn(pe, pre.plus(1), "turn x")
            s1_pe_fn(pe, pre.plus(1), "project first pair")
            max_turn(PRO_USES - 1, 2 + (PRO_USES - 1) % 2, PRO_USES - 2, 0)
            s1_pe_fn(pe, pre.plus(1), "project second pair")
            s1_pe_fn(pe, pre.plus(1), "project q")

            def scores_T(G, n, b, c):
                q = n * NC + c
                if c == 0:
                    pe.wait_ge(mrow_in, (n + 1) * 16)
                if due(q - 1):
                    pe.wait_ge(exp_done, q - 1)
                pe.matmul(bank[4 + c % 2][:], ctxT[:, G.parity, b * S:(b + 1) * S],
                          Y[:, b, c * CH:(c + 1) * CH, :], start=True, stop=True).then_inc(st_ready, 1)

            def z_product(G, n, b, c):
                q = n * NC + c
                count, bk = z_use(G, b, f"z{c}")
                pe.wait_ge(exp_done, q + 1)
                pe.wait_ge(z_evac, count - 1)
                pe.matmul(bank[bk][0:DE + 1, :], ctx_nat[:, G.parity, b, :],
                          pT[:, b % 2, c * CH * S:(c + 1) * CH * S], start=True, stop=True).then_inc(z_ready, 1)

            def out_product(count, bk, n, b):
                pe.wait_ge(rot_free, count - 1)
                for h in range(XH):
                    if h % CH == 0:
                        pe.wait_ge(norm_done, n * NC + h // CH + 1)
                    last = pe.matmul(bank[bk][:, 0:D], zs[0:DE, b % 2, h * S:(h + 1) * S], Bw[:, h, :],
                                     start=(h == 0), stop=(h == XH - 1))
                last.then_inc(rot_ready, 1)

            def ffn(G, b, m, i):
                r = b % 2
                count, bk = use_index(G, b, "f", i)
                ps = bank[bk]
                pe.wait_ge(rot_free, count - 1)
                if i == 1 and isinstance(m, int) and m == 0:
                    pe.wait_ge(wm_in, 16 * 7)
                if i == 0:
                    pe.wait_ge(s3_h3, m + 1)
                    last = pe.transpose(ps[:, 0:S], h3[:, r, :], ident[:])
                if i == 1:
                    pe.wait_ge(rot_free, use_index(G, b, "f", 0)[0] + 1)
                    last = pe.matmul(ps[:, 0:E], h3T[:], gate[:], start=True, stop=True)
                if i == 2:
                    last = pe.matmul(ps[:], h3T[:], sh_gu[:], start=True, stop=True)
                if i == 3:
                    pe.wait_ge(s3_oh, m + 1)
                    pe.matmul(ps[:, 0:E], before[:], onehot[:], start=True, stop=True)
                    last = pe.matmul(ps[:, E:2 * E], ones16[:], onehot[:], start=True, stop=True)
                if i == 4:
                    pe.wait_ge(rot_free, use_index(G, b, "f", 2)[0] + 1)
                    for k in range(I // P):
                        last = pe.transpose(ps[:, k * P:(k + 1) * P], act3[:, k * P:(k + 1) * P], ident[:])
                if i == 5:
                    pe.wait_ge(rot_free, use_index(G, b, "f", 4)[0] + 1)
                    for k in range(I // P):
                        last = pe.matmul(ps[:, 0:D], act3T[:, k * P:(k + 1) * P], sh_dn[:, k, :],
                                         start=(k == 0), stop=(k == I // P - 1))
                last.then_inc(rot_ready, 1)

            def body(G, slots):
                for b in range(slots):
                    n = G.number * GB + b
                    f = (lambda i: ffn(G, b, n - 2, i)) if does(n, "ffn") else (lambda i: None)
                    st = (lambda c: scores_T(G, n, b, c)) if does(n, "scores") else (lambda c: None)
                    z = (lambda c: z_product(G, n, b, c)) if does(n, "scores") else (lambda c: None)
                    s1 = lambda place: s1_step(s1_pe_fn, pe, PE_STEPS, G, b, place)

                    def y(kind, i):
                        if has_y(n, b):
                            source = G if b == 0 else G.plus(1)
                            half = 1 if b == 0 else 0
                            if kind == "act" and i == 0:
                                pe.wait_ge(*consumed(source, 12))
                            if kind == "dve":
                                y_product(*use_index(G, b, "y", i), source, half, 2 * i)
                            else:
                                y_product(*z_use(G, b, f"y{i}"), source, half, 2 * i + 1, z_evac, z_ready)

                    def rows(c):
                        if does(n, "max"):
                            if c == 0:
                                pe.wait_ge(rot_free, base(G.number, b))
                                pe.wait_ge(z_evac, z_base(G, b))
                                if b == 3:
                                    pe.wait_ge(*consumed(G.plus(1), 13))
                            score_rows(*use_index(G, b, "stm", c), (G.parity + (b == 3)) % 2, b + 1, c)

                    st(0)
                    rows(0)
                    rows(1)
                    st(1)
                    rows(2)
                    z(0)
                    rows(3)
                    s1("A")
                    st(2)
                    f(0)
                    if does(n, "max"):
                        max_turn(*use_index(G, b, "mt"), use_index(G, b, "stm", NC - 1)[0], b + 1)
                    z(1)
                    s1("B")
                    f(1)
                    f(2)
                    st(3)
                    y("act", 0)
                    y("dve", 0)
                    y("act", 1)
                    y("dve", 1)
                    f(3)
                    z(2)
                    s1("C")
                    y("dve", 2)
                    y("act", 2)
                    y("dve", 3)
                    y("act", 3)
                    f(4)
                    z(3)
                    s1("D")
                    f(5)
                    if does(n, "out"):
                        out_product(*use_index(G, b, "out"), n - 1, b + 1)

            over_groups(pe, body)

            pe.wait_ge(table, TABLE_CHAIN)
            pe.wait_ge(rot_free, base(NG, SLOTS - B))

            def expert_of(j):
                at = exp_tab[0:1, j:j + 1] if isinstance(j, int) else exp_tab[0:1, bass.ds(j, 1)]
                return pe.value_load(at, min_val=0, max_val=E - 1)

            held = {}

            def step(j, k, turn):
                if tile_runs(j, 0):
                    r = k % RING
                    pe.wait_ge(rec_in[r], 16 * (turn + 1))
                    pe.transpose(bank[k % 2][:, 0:P], rec[:, r, 0:D], ident[:]).then_inc(ft_ready, 1)
                if tile_runs(j, 1):
                    if k == 0:
                        held.clear()
                        held[-1] = expert_of(j - 1)
                    e = held[k - 1]
                    pe.wait_ge(ft_copied, j)
                    pe.matmul(bank[2 + (k - 1) % 2][:], recT[:, (k - 1) % 2], rt_gu[:, bass.ds(e * (2 * I), 2 * I)],
                              start=True, stop=True).then_inc(gu_ready, 1)
                if tile_runs(j, 0) and k < RING - 1:
                    held[k] = expert_of(j)
                if tile_runs(j, 3) and k < 2:
                    held[k - 3] = expert_of(j - 3)
                if tile_runs(j, 2):
                    pe.wait_ge(act_done, j - 1)
                    for h in range(I // P):
                        last = pe.transpose(bank[4 + k % 2][:, h * P:(h + 1) * P],
                                            act4[:, k % 2, h * P:(h + 1) * P], ident[:])
                    last.then_inc(at_ready, 1)
                if tile_runs(j, 3):
                    e = held[k - 3]
                    pe.wait_ge(at_copied, j - 2)
                    if due(j - 4):
                        pe.wait_ge(y_done, j - 4)
                    for h in range(I // P):
                        last = pe.matmul(bank[6 + (k - 3) % 2][:, 0:D], act4T[:, (k - 3) % 2, h * P:(h + 1) * P],
                                         rt_dn[:, bass.ds(e * I + h * P, P)], start=(h == 0),
                                         stop=(h == I // P - 1))
                    last.then_inc(dn_ready, 1)

            over_tiles(pe, step)


_INS = ['x', 'ctx_768', 'L0_attn_Wh', 'L0_attn_bh', 'L0_attn_Wq', 'L0_attn_bq', 'L0_attn_Wk', 'L0_attn_bk',
        'L0_attn_Wv', 'L0_attn_bv', 'L0_attn_beta', 'L0_attn_ln_w', 'L0_attn_ln_b', 'L0_attn_Wo', 'L0_attn_bo',
        'L0_xattn_Wq', 'L0_xattn_Wk', 'L0_xattn_Wv', 'L0_xattn_Wo', 'L0_xattn_bo', 'L0_ffn_gate_w',
        'L0_ffn_sh_gate', 'L0_ffn_sh_up', 'L0_ffn_sh_down', 'L0_ffn_rt_gate', 'L0_ffn_rt_up', 'L0_ffn_rt_down']


def kernel(**inputs):
    import numpy as _np
    import concourse.bacc as _bacc
    from concourse import mybir as _mybir
    from concourse.bass_utils import run_bass_kernel_spmd as _run

    nc = _bacc.Bacc("TRN2", target_bir_lowering=False, num_devices=1)
    arrays, args = {}, []
    for name in _INS:
        a = _np.ascontiguousarray(inputs[name])
        arrays[f"in_{name}_dram"] = a
        args.append(nc.dram_tensor(f"in_{name}_dram", a.shape, _mybir.dt.from_np(a.dtype), kind="ExternalInput").ap())
    batch, tokens, width = inputs['x'].shape
    experts = inputs['L0_ffn_gate_w'].shape[1]
    heads = inputs['L0_xattn_Wq'].shape[1] // 64
    f32 = _mybir.dt.float32
    r_scratch = nc.dram_tensor("r_scratch", (batch, heads * tokens), f32, kind="Internal").ap()
    routed = nc.dram_tensor("routed", (experts * (batch * tokens + 128) + 128, 2 * width + 1), f32,
                            kind="Internal").ap()
    out = nc.dram_tensor("out_0_dram", (batch, tokens, width), f32, kind="ExternalOutput").ap()
    decoder_layer(nc, *args, r_scratch, routed, out)
    r = _run(nc, [arrays], core_ids=[0])
    return r.results[0]["out_0_dram"]
```
